# Optimizing a Trainium2 kernel written in Bass

```python
import numpy as np
import jax
import jax.numpy as jnp

def _softmax(x, axis=-1):
    return jax.nn.softmax(x, axis=axis)

def _gelu(x):
    return jax.nn.gelu(x, approximate=True)

def _silu(x):
    return jax.nn.silu(x)

def _sigmoid(x):
    return jax.nn.sigmoid(x)

def _layernorm(x, axis=-1, eps=1e-05):
    m = jnp.mean(x, axis=axis, keepdims=True)
    v = jnp.var(x, axis=axis, keepdims=True)
    return (x - m) / jnp.sqrt(v + eps)

def _scatter_add(tgt, idx, src, axis=0):
    return tgt.at[idx].add(src)

def _segment_sum(src, seg, n):
    return jax.ops.segment_sum(src, seg, n)
kernel_name = 'mk_flamingo_gated_d1_seqx_r4_a355f2'

def setup_inputs(seed: int=0):
    np.random.seed(seed)
    _w = jnp.asarray

    def _rec_inputs():
        import jax
        import jax.numpy as jnp
        _rk = jax.random.key(seed)
        x = -0.0002928 + 1 * jax.random.normal(jax.random.fold_in(_rk, 1), (8, 512, 256), jnp.float32)
        _lenS = 512 - jax.random.randint(jax.random.fold_in(_rk, 7), (8,), 0, max(1, 512 // 4) + 1, jnp.int32)
        _lenS2 = 512 - jax.random.randint(jax.random.fold_in(_rk, 8), (8,), 0, max(1, 512 // 4) + 1, jnp.int32)
        _ctx_1024P = jax.random.normal(jax.random.fold_in(_rk, 11), (8, 16, 256), jnp.float32)
        _ctx_1024c = jax.random.dirichlet(jax.random.fold_in(_rk, 511), 0.3 * jnp.ones((16,), jnp.float32), (8, 512))
        _ctx_1024t = jnp.einsum('bsk,bkd->bsd', _ctx_1024c, _ctx_1024P)
        _ctx_1024t = _ctx_1024t * jax.lax.rsqrt(jnp.mean(jnp.square(_ctx_1024t)) + 1e-12) * 0.953939
        ctx_1024 = -1.39393e-06 + 0.999914 * (_ctx_1024t + 0.3 * jax.random.normal(jax.random.fold_in(_rk, 611), (8, 512, 256), jnp.float32))
        _validS = jnp.arange(512)[None, :] < _lenS[:, None]
        _validS2 = jnp.arange(512)[None, :] < _lenS2[:, None]
        _causal = jnp.tril(jnp.ones((512, 512), dtype=bool))
        mask_BxS2_bk1 = jnp.broadcast_to(_validS2[:, :], (8, 512))
        _g = jax.random.normal(jax.random.fold_in(_rk, 9001), (2, 1), jnp.float32)
        _g = jnp.sign(_g) * jnp.maximum(jnp.abs(_g), 1.0) + (_g == 0) * 1.0
        g_xattn = _g[0]
        g_ffn = _g[1]
        return (x, ctx_1024, mask_BxS2_bk1, g_xattn, g_ffn)
    x, ctx_1024, mask_BxS2_bk1, g_xattn, g_ffn = _rec_inputs()

    def _L0_xattn_setup():
        import jax, jax.numpy as jnp
        import numpy as np
        B, S, D, H = (2, 512, 256, 16)
        DH = D // H
        key = jax.random.key(seed)
        ks = jax.random.split(key, 16)
        inp = {'query': jax.random.normal(ks[0], (B, S, D), jnp.float32), 'key': jax.random.normal(ks[1], (B, S, D), jnp.float32), 'value': jax.random.normal(ks[2], (B, S, D), jnp.float32), 'key_padding_mask': jnp.arange(S)[None, :] < jnp.array([S, S - 64])[:, None], 'relative_bias': jax.random.normal(ks[3], (1, H, S, S), jnp.float32) * 0.1}
        sc = 1.0 / np.sqrt(D)
        for i, n in enumerate(['q', 'k', 'v', 'o']):
            inp[f'W{n}'] = jax.random.normal(ks[4 + 2 * i], (D, D), jnp.float32) * sc
            inp[f'b{n}'] = jnp.zeros((D,), jnp.float32)
        return inp
    _L0_xattn_all = _L0_xattn_setup()
    _L0_xattn_in = {k: v for k, v in _L0_xattn_all.items() if k in ('relative_bias', 'Wq', 'bq', 'Wk', 'bk', 'Wv', 'bv', 'Wo', 'bo')}
    del _L0_xattn_all

    def _L0_ffn_setup():
        import jax, jax.numpy as jnp
        import numpy as np
        D_MODEL, D_FF, RANK = (256, 1024, 64)
        B, S = (4, 1024)
        key = jax.random.key(seed)
        ks = jax.random.split(key, 7)
        return {'x': jax.random.normal(ks[0], (B, S, D_MODEL), dtype=jnp.float32), 'U1': jax.random.normal(ks[1], (D_MODEL, RANK), dtype=jnp.float32) * 0.02, 'V1': jax.random.normal(ks[2], (RANK, D_FF), dtype=jnp.float32) * 0.02, 'b1': jnp.zeros((D_FF,), dtype=jnp.float32), 'U2': jax.random.normal(ks[3], (D_FF, RANK), dtype=jnp.float32) * 0.02, 'V2': jax.random.normal(ks[4], (RANK, D_MODEL), dtype=jnp.float32) * 0.02, 'b2': jnp.zeros((D_MODEL,), dtype=jnp.float32)}
    _L0_ffn_all = _L0_ffn_setup()
    _L0_ffn_in = {k: v for k, v in _L0_ffn_all.items() if k in ('U1', 'V1', 'b1', 'U2', 'V2', 'b2')}
    del _L0_ffn_all
    return {'x': x, 'ctx_1024': ctx_1024, 'mask_BxS2_bk1': mask_BxS2_bk1, 'g_xattn': g_xattn, 'g_ffn': g_ffn, 'L0_xattn_relative_bias': _L0_xattn_in['relative_bias'], 'L0_xattn_Wq': _L0_xattn_in['Wq'], 'L0_xattn_bq': _L0_xattn_in['bq'], 'L0_xattn_Wk': _L0_xattn_in['Wk'], 'L0_xattn_bk': _L0_xattn_in['bk'], 'L0_xattn_Wv': _L0_xattn_in['Wv'], 'L0_xattn_bv': _L0_xattn_in['bv'], 'L0_xattn_Wo': _L0_xattn_in['Wo'], 'L0_xattn_bo': _L0_xattn_in['bo'], 'L0_ffn_U1': _L0_ffn_in['U1'], 'L0_ffn_V1': _L0_ffn_in['V1'], 'L0_ffn_b1': _L0_ffn_in['b1'], 'L0_ffn_U2': _L0_ffn_in['U2'], 'L0_ffn_V2': _L0_ffn_in['V2'], 'L0_ffn_b2': _L0_ffn_in['b2']}

def reference(x, ctx_1024, mask_BxS2_bk1, g_xattn, g_ffn, L0_xattn_relative_bias, L0_xattn_Wq, L0_xattn_bq, L0_xattn_Wk, L0_xattn_bk, L0_xattn_Wv, L0_xattn_bv, L0_xattn_Wo, L0_xattn_bo, L0_ffn_U1, L0_ffn_V1, L0_ffn_b1, L0_ffn_U2, L0_ffn_V2, L0_ffn_b2):
    import jax
    import jax.numpy as jnp

    def _L0_xattn_ref(query, key, value, key_padding_mask, relative_bias, Wq, bq, Wk, bk, Wv, bv, Wo, bo):
        import jax, jax.numpy as jnp
        import numpy as np
        B, S, D, H = (2, 512, 256, 16)
        DH = D // H

        def split_heads(x):
            b, s, _ = x.shape
            return x.reshape(b, s, H, DH).transpose(0, 2, 1, 3)
        q = split_heads(query @ Wq.T + bq)
        k = split_heads(key @ Wk.T + bk)
        v = split_heads(value @ Wv.T + bv)
        scores = jnp.einsum('bhqd,bhkd->bhqk', q, k) / jnp.sqrt(jnp.asarray(DH, q.dtype))
        scores = scores + relative_bias
        scores = jnp.where(key_padding_mask[:, None, None, :], scores, -jnp.inf)
        attn = jax.nn.softmax(scores, axis=-1)
        out = jnp.einsum('bhqk,bhkd->bhqd', attn, v)
        out = out.transpose(0, 2, 1, 3).reshape(query.shape[0], query.shape[1], D)
        return out @ Wo.T + bo

    def _L0_ffn_ref(x, U1, V1, b1, U2, V2, b2):
        import jax, jax.numpy as jnp
        import numpy as np
        D_MODEL, D_FF, RANK = (256, 1024, 64)
        B, S = (4, 1024)
        P = jnp.einsum('bsd,dr->bsr', x, U1)
        H = jax.nn.gelu(jnp.einsum('bsr,rf->bsf', P, V1) + b1)
        Q = jnp.einsum('bsf,fr->bsr', H, U2)
        return jnp.einsum('bsr,rd->bsd', Q, V2) + b2
    x = x + jnp.tanh(g_xattn[0]) * _L0_xattn_ref(_layernorm(x, axis=-1), ctx_1024, ctx_1024, mask_BxS2_bk1, L0_xattn_relative_bias, L0_xattn_Wq, L0_xattn_bq, L0_xattn_Wk, L0_xattn_bk, L0_xattn_Wv, L0_xattn_bv, L0_xattn_Wo, L0_xattn_bo)
    x = x + jnp.tanh(g_ffn[0]) * _L0_ffn_ref(_layernorm(x, axis=-1), L0_ffn_U1, L0_ffn_V1, L0_ffn_b1, L0_ffn_U2, L0_ffn_V2, L0_ffn_b2)
    return x

_drawn_inputs = setup_inputs


def setup_inputs(seed=0):
    import zlib

    import numpy as np

    out = dict(_drawn_inputs(seed))
    spreads = {'L0_xattn_bq': (0.0, 0.498),
     'L0_xattn_bk': (0.0, 2.0),
     'L0_xattn_bv': (0.0, 0.1),
     'L0_xattn_bo': (0.0, 0.1),
     'L0_ffn_b1': (0.0, 0.8),
     'L0_ffn_b2': (0.0, 0.8)}
    factors = {'L0_xattn_relative_bias': 8.0,
     'L0_ffn_U1': 8.0,
     'L0_ffn_V1': 8.0,
     'L0_ffn_U2': 8.0,
     'L0_ffn_V2': 8.0}
    for name, (base, spread) in spreads.items():
        noise = np.random.default_rng([zlib.crc32(name.encode()), seed]).standard_normal(out[name].shape)
        drawn = base * np.exp(spread * noise) if base else spread * noise
        out[name] = jnp.asarray(drawn.astype(out[name].dtype))
    for name, factor in factors.items():
        out[name] = (out[name] * factor).astype(out[name].dtype)
    return out
```

```python
from contextlib import ExitStack

import concourse.bass as bass
from concourse import mybir

F32 = mybir.dt.float32
BF16 = mybir.dt.bfloat16
U8 = mybir.dt.uint8
ALU = mybir.AluOpType
ACT = mybir.ActivationFunctionType

P = 128
B, S, D = 8, 512, 256
H, DH = 16, 16
J = D // P
TT = S // P
FF, RANK = 1024, 64
FJ = FF // P
HPJ = P // DH
TERMS = 6
ROWS = TERMS * DH
QUERY_PARTS = [(0, 3), (1, 2), (2, 1)]
KEY_PARTS = [(0, 3), (0, 2), (0, 1)]
MASKED = 1.0e30
LOWEST = -3.0e38
EPS = 1.0e-5
SCALE = DH ** -0.5
GROUP = 4
VW = 32
SLOTS = 2 * B
TURNS = H // 2
PV_FREE = 4
O_STORES = 16 * (GROUP + 1)
STACKS = 16 * (len(QUERY_PARTS) + len(KEY_PARTS))
BATCH_LOADS = 16 * (J + 2)
T_FREE = 4
MROW = ROWS
CONST_LOADS = 16 * 14
BARRIER = 5


def flamingo_kernel(nc, x, ctx_in, mask, g_xattn, g_ffn, rel_bias, Wq, bq, Wk, bk, Wv, bv, Wo, bo,
                    U1, V1, b1, U2, V2, b2, out, qk_parts, values_raw, sums, recips):
    with ExitStack() as ctx:
        def sb(name, shape, dt=F32):
            return ctx.enter_context(nc.sbuf_tensor(name, shape, dt))

        def sem(name):
            return ctx.enter_context(nc.semaphore(name))

        ps = ctx.enter_context(nc.psum_tensor("ps", [P, 8, 512], F32))

        ident = sb("ident", [P, P])
        wT = sb("wT", [P, 4, J, D])
        u1_sb = sb("u1_sb", [P, J, RANK])
        v1_sb = sb("v1_sb", [RANK, FF])
        u2_sb = sb("u2_sb", [P, FJ, RANK])
        v2_sb = sb("v2_sb", [P, D])
        b1_col = sb("b1_col", [P, FJ])
        qkv_b = sb("qkv_b", [P, 3, J])
        row_b = sb("row_b", [P, 2, D])
        gates = sb("gates", [P, 2])
        eps4 = sb("eps4", [P, 2, TT])
        stats = sb("stats", [P, TT, 6])
        mv = sb("mv", [P, TT, 2])
        rstd = sb("rstd", [P, TT])

        v_all = sb("v_all", [P, H, B * TT, DH])
        bias_sb = sb("bias_sb", [P, 2, TT, S])
        q_st = sb("q_st", [P, 2, B * S], BF16)
        k_st = sb("k_st", [P, 2, B * S], BF16)
        t_sb = sb("t_sb", [P, 2, TT, S])
        p_sb = sb("p_sb", [P, B, TT, S])
        v_win = sb("v_win", [P, 2, B * TT, VW])
        o_sb = sb("o_sb", [P, 2, S])
        mx = sb("mx", [P, 2, TT])

        arena = p_sb[:, :, :, :].rearrange("p b t s -> p (b t s)")

        def at(lo, n):
            return arena[:, lo:lo + n]

        x_in = at(0, 2048).rearrange("p (u t d) -> p u t d", u=2, t=TT)
        c_in = at(2048, 2048).rearrange("p (u t d) -> p u t d", u=2, t=TT)
        xT = at(4096, 1024).rearrange("p (j s) -> p j s", j=J)
        cT = at(5120, 1024).rearrange("p (j s) -> p j s", j=J)
        zf = at(6144, 2048).rearrange("p (z j s) -> p z j s", z=2, j=J)
        parts = at(8192, 6144).bitcast(BF16).rearrange("p (z u k s) -> p z u k s", z=2, u=2, k=3 * J)
        w_raw = t_sb[:, 0, :, :].rearrange("p w (j d) -> p w j d", j=J)
        mask_u8 = t_sb[:, 1, 0:2, :].rearrange("p a s -> p (a s)").bitcast(U8)
        n_in = at(0, 2048).rearrange("p (u j s) -> p u j s", u=2, j=J)
        r_in = at(2048, 2048).rearrange("p (u j s) -> p u j s", u=2, j=J)
        x3 = at(4096, 2048).rearrange("p (u t d) -> p u t d", u=2, t=TT)
        x1 = at(6144, 2048).rearrange("p (u t d) -> p u t d", u=2, t=TT)
        xn3 = at(8192, 1024).rearrange("p (t d) -> p t d", t=TT)
        xnT = at(9216, 1024).rearrange("p (j s) -> p j s", j=J)
        pT = at(10240, 512)
        hT = at(10752, 4096).rearrange("p (f s) -> p f s", f=FJ)
        rT = at(14848, 512)
        y_out = t_sb[:, 0, :, :].rearrange("p t (u d) -> p u t d", u=2)
        dens = t_sb[:, 1, 0, :]

        passed_sp = sem("passed_sp")
        passed_dve = sem("passed_dve")
        weights_in = sem("weights_in")
        consts_in = sem("consts_in")
        made_consts = sem("made_consts")
        wt_done = sem("wt_done")
        wt_copied = sem("wt_copied")
        ident_zero = sem("ident_zero")
        ident_done = sem("ident_done")
        gates_done = sem("gates_done")
        win_zero = sem("win_zero")
        mask_done = sem("mask_done")
        x_loaded = [sem(f"x_loaded{u}") for u in range(2)]
        c_loaded = [sem(f"c_loaded{u}") for u in range(2)]
        ctx_turned = sem("ctx_turned")
        x_turned = sem("x_turned")
        v_done = sem("v_done")
        k_done = sem("k_done")
        q_done = sem("q_done")
        ctx_copied = sem("ctx_copied")
        v_copied = sem("v_copied")
        k_copied = sem("k_copied")
        q_copied = sem("q_copied")
        x_copied = sem("x_copied")
        half_stats = sem("half_stats")
        moments = sem("moments")
        var_eps = sem("var_eps")
        rstd_done = sem("rstd_done")
        xn_done = sem("xn_done")
        split_done = [sem("q_split"), sem("k_split")]
        rest_done = sem("rest_done")
        middle_done = sem("middle_done")
        parts_stored = [[sem(f"parts_stored{z}{u}") for u in range(2)] for z in range(2)]
        phase_end = sem("phase_end")

        stack_in = [sem(f"stack_in{u}") for u in range(2)]
        bias_in = [sem(f"bias_in{u}") for u in range(2)]
        scores_done = sem("scores_done")
        biased = sem("biased")
        lowered_pool = sem("lowered_pool")
        lowered_dve = sem("lowered_dve")
        turned = sem("turned")
        exp_done = sem("exp_done")
        v_window = sem("v_window")
        pv_done = sem("pv_done")
        o_copied = sem("o_copied")
        o_stored = [sem(f"o_stored{u}") for u in range(2)]

        dens_in = sem("dens_in")
        recip_done = sem("recip_done")
        recip_out = sem("recip_out")
        n_loaded = [sem(f"n_loaded{u}") for u in range(2)]
        o_scaled = sem("o_scaled")
        o_ready = sem("o_ready")
        x_biased = sem("x_biased")
        proj_done = sem("proj_done")
        x1_done = sem("x1_done")
        half_stats3 = sem("half_stats3")
        moments3 = sem("moments3")
        var_eps3 = sem("var_eps3")
        rstd3 = sem("rstd3")
        xn3_done = sem("xn3_done")
        xn3_turned = sem("xn3_turned")
        xnT_copied = sem("xnT_copied")
        rank_done = sem("rank_done")
        rank_copied = sem("rank_copied")
        ff_done = sem("ff_done")
        gelu_done = sem("gelu_done")
        down_done = sem("down_done")
        down_copied = sem("down_copied")
        ffn_done = sem("ffn_done")
        x1_biased = sem("x1_biased")
        y_done = sem("y_done")
        y_stored = [sem(f"y_stored{u}") for u in range(2)]

        mask_row = mask.rearrange("b s -> (b s)").rearrange("(a s) -> a s", a=1)
        x_v = x.rearrange("b (t p) d -> b p t d", p=P)
        c_v = ctx_in.rearrange("b (t p) d -> b p t d", p=P)
        out_v = out.rearrange("b (t p) d -> b p t d", p=P)
        bias_v = rel_bias.rearrange("o h (t p) k -> (o h) p t k", p=P)
        parts_v = qk_parts.rearrange("z k (j p) s -> z p (k j) s", p=P)
        values_v = values_raw.rearrange("b (j p) s -> b p j s", p=P)
        recip_v = recips.rearrange("b (j h o) s -> b j h o s", j=J, o=1)

        def turns(eng, n, body):
            with eng.Fori(0, n - 1) as i:
                body(i, False)
            body(n - 1, True)

        block = ctx.enter_context(nc.Block())

        @block.sync
        def _(sp):
            for w, src in enumerate((Wq, Wk, Wv, Wo)):
                sp.dma_start(w_raw[:, w], src.rearrange("(j p) d -> p j d", p=P)).then_inc(weights_in, 16)
            for u in range(2):
                sp.dma_start(c_in[:, u], c_v[u]).then_inc(c_loaded[u], 16)
                sp.dma_start(x_in[:, u], x_v[u]).then_inc(x_loaded[u], 16)

            def project(i, last):
                for u in range(2):
                    b = 2 * i + u
                    for z, done in ((1, split_done[1]), (0, split_done[0])):
                        sp.wait_ge(done, b + 2)
                        sp.sem_inc(passed_sp, 1)
                        sp.dma_start(parts_v[z][:, :, bass.ds(b * S, S)], parts[:, z, u]).then_inc(parts_stored[z][u], 16)
                        if z == 1 and not last:
                            sp.wait_ge(ctx_turned, b + 1)
                            sp.dma_start(c_in[:, u], c_v[bass.ds(b + 2, 1)].rearrange("o p t d -> (o p) t d")).then_inc(c_loaded[u], 16)
                            sp.wait_ge(x_turned, b + 1)
                            sp.dma_start(x_in[:, u], x_v[bass.ds(b + 2, 1)].rearrange("o p t d -> (o p) t d")).then_inc(x_loaded[u], 16)

            turns(sp, B // 2, project)
            for z in range(2):
                for u in range(2):
                    sp.wait_ge(parts_stored[z][u], 16 + 16 * (B // 2))
            sp.sem_inc(phase_end, 1)
            sp.wait_ge(phase_end, BARRIER)

            def load_head(h, u):
                sp.dma_start(bias_sb[:, u], bias_v[bass.ds(h, 1)].rearrange("o p t k -> (o p) t k")).then_inc(bias_in[u], 16)
                rows = bass.ds(h * DH, DH)
                row = 0
                for part, times in QUERY_PARTS:
                    src = qk_parts[0, part:part + 1, rows, :].broadcast_to([times, DH, B * S])
                    sp.dma_start(q_st[row:row + times * DH, u, :], src).then_inc(stack_in[u], 16)
                    row += times * DH
                row = 0
                for part, n in KEY_PARTS:
                    sp.dma_start(k_st[row:row + n * DH, u, :], qk_parts[1, part:part + n, rows, :]).then_inc(stack_in[u], 16)
                    row += n * DH

            load_head(0, 0)
            load_head(1, 1)

            def attend(i, last):
                for u in range(2):
                    for half in range(2):
                        k = 4 * i + 2 * u + half
                        sp.wait_ge(o_copied, k + 3)
                        for g in range(GROUP):
                            sp.dma_start(values_raw[GROUP * half + g, bass.ds((2 * i + u) * DH, DH), :],
                                         o_sb[VW * g:VW * g + DH, half, :]).then_inc(o_stored[half], 16)
                        sp.dma_start(sums[GROUP * half:GROUP * (half + 1), bass.ds(2 * i + u, 1), :].rearrange("b h s -> (b h) s"),
                                     o_sb[DH:P:VW, half, :]).then_inc(o_stored[half], 16)
                        if half == 0 and not last:
                            sp.wait_ge(biased, 4 * B * (2 * i + u + 1))
                            load_head(2 * i + u + 2, u)

            turns(sp, TURNS, attend)
            for u in range(2):
                sp.wait_ge(o_stored[u], O_STORES * (H + 1))
            sp.sem_inc(phase_end, 1)
            sp.wait_ge(phase_end, 2 * BARRIER)

            sp.dma_start(dens, sums.rearrange("b h s -> (b h) s")).then_inc(dens_in, 16)
            sp.wait_ge(recip_done, 1)
            sp.dma_start(recips.rearrange("b h s -> (b h) s"), dens).then_inc(recip_out, 16)
            sp.wait_ge(recip_out, 16)

            def load_batch(b, u):
                sp.dma_start(n_in[:, u], values_v[bass.ds(b, 1)].rearrange("o p j s -> (o p) j s")).then_inc(n_loaded[u], 16)
                for j in range(J):
                    src = recip_v[bass.ds(b, 1), j].rearrange("b h o s -> (b h) o s").broadcast_to([HPJ, DH, S])
                    sp.dma_start(r_in[:, u, j, :], src).then_inc(n_loaded[u], 16)
                sp.dma_start(x3[:, u], x_v[bass.ds(b, 1)].rearrange("o p t d -> (o p) t d")).then_inc(n_loaded[u], 16)

            load_batch(0, 0)
            load_batch(1, 1)

            def finish(i, last):
                for u in range(2):
                    b = 2 * i + u
                    if not last:
                        sp.wait_ge(x1_done, b + 1)
                        sp.wait_ge(o_ready, b + 1)
                        load_batch(b + 2, u)
                    sp.wait_ge(y_done, b + 2)
                    sp.dma_start(out_v[bass.ds(b, 1)].rearrange("o p t d -> (o p) t d"), y_out[:, u]).then_inc(y_stored[u], 16)

            turns(sp, B // 2, finish)
            for u in range(2):
                sp.wait_ge(y_stored[u], 16 * (B // 2 + 1))
            sp.wait_ge(consts_in, CONST_LOADS)

        @block.gpsimd
        def _(pool):
            for s, n in ((v_copied, 1), (k_copied, 1), (q_copied, 1), (x_copied, 1), (split_done[0], 1), (split_done[1], 1),
                         (o_copied, 2), (turned, T_FREE), (pv_done, PV_FREE), (gelu_done, 2), (down_copied, 1), (y_done, 1)):
                pool.sem_inc(s, n)
            for u in range(2):
                for z in range(2):
                    pool.sem_inc(parts_stored[z][u], 16)
                pool.sem_inc(o_stored[u], O_STORES)
                pool.sem_inc(y_stored[u], 16)
            nc.gpsimd.memset(ident[:, :], 0.0).then_inc(ident_zero, 1)
            pool.wait_ge(ident_zero, 1)
            nc.gpsimd.affine_select(out=ident[:, :], in_=ident[:, :], compare_op=ALU.not_equal, fill=1.0, base=0,
                                    pattern=[[-1, P]], channel_multiplier=1).then_inc(ident_done, 1)
            nc.gpsimd.memset(eps4[:, 0, :], EPS)
            nc.gpsimd.memset(eps4[:, 1, :], -0.5)
            for u in range(2):
                nc.gpsimd.memset(v_win[:, u], 0.0).then_inc(win_zero, 1)
            pool.wait_ge(win_zero, 2)
            nc.gpsimd.memset(v_win[:, :, :, DH:DH + 1], 1.0).then_inc(win_zero, 1)
            pool.wait_ge(win_zero, 3)

            def reciprocal_root(out_ap, var, done_eps, n, done):
                nc.gpsimd.tensor_tensor(out_ap, var, eps4[:, 0, :], ALU.add).then_inc(done_eps, 1)
                pool.wait_ge(done_eps, n)
                nc.gpsimd.tensor_tensor(out_ap, out_ap, eps4[:, 1, :], ALU.pow).then_inc(done, 1)

            with pool.Fori(0, B) as b:
                pool.wait_ge(moments, b + 1)
                reciprocal_root(rstd[:, :], mv[:, :, 1], var_eps, b + 1, rstd_done)
            pool.drain().then_inc(phase_end, 1)
            pool.wait_ge(phase_end, BARRIER)

            def attend(i, last):
                for s in range(SLOTS):
                    u, w = s // B, s % 2
                    if s % B == 0:
                        pool.wait_ge(pv_done, 4 * i + 2 * u + 2)
                        nc.gpsimd.tensor_copy(v_win[:, u, :, 0:DH], v_all[:, bass.ds(2 * i + u, 1), :, :].rearrange("p o t d -> p (o t) d")).then_inc(v_window, 1)
                    for t in range(1, TT):
                        pool.wait_ge(biased, 4 * (SLOTS * i + s) + t + 1)
                        ins = nc.gpsimd.tensor_tensor(t_sb[:, w, t, :], t_sb[:, w, t, :], mx[:, w, t:t + 1].broadcast_to([P, S]), ALU.subtract)
                    ins.then_inc(lowered_pool, 1)

            turns(pool, TURNS, attend)
            pool.drain().then_inc(phase_end, 1)
            pool.wait_ge(phase_end, 2 * BARRIER)

            def value_bias(b, i, u):
                pool.wait_ge(o_scaled, b + 1)
                bias = qkv_b[:, 2, :].rearrange("p (j o) -> p j o", o=1).broadcast_to([P, J, S])
                nc.gpsimd.tensor_tensor(n_in[:, u], n_in[:, u], bias, ALU.add).then_inc(o_ready, 1)

            def bias_tokens(b, i, u):
                pool.wait_ge(n_loaded[u], BATCH_LOADS * (i + 1))
                row = row_b[:, 0:1, :].broadcast_to([P, TT, D])
                nc.gpsimd.tensor_tensor(x3[:, u], x3[:, u], row, ALU.add).then_inc(x_biased, 1)

            def after_attention(b, u):
                pool.wait_ge(moments3, b + 1)
                reciprocal_root(rstd[:, :], mv[:, :, 1], var_eps3, b + 1, rstd3)
                pool.wait_ge(xn3_done, b + 1)
                row = row_b[:, 1:2, :].broadcast_to([P, TT, D])
                nc.gpsimd.tensor_tensor(x1[:, u], x1[:, u], row, ALU.add).then_inc(x1_biased, 1)

            value_bias(0, 0, 0)
            bias_tokens(0, 0, 0)
            value_bias(1, 0, 1)
            after_attention(0, 0)

            def finish(i, last):
                for u in range(2):
                    b, v = 2 * i + u, 1 - u
                    if not (last and u == 1):
                        bias_tokens(b + 1, i + u, v)
                        after_attention(b + 1, v)
                    if not last:
                        value_bias(b + 2, i + 1, u)

            turns(pool, B // 2, finish)

        @block.scalar
        def _(act):
            loads = [(qkv_b[:, n, :], v.rearrange("(j p) -> p j", p=P)) for n, v in enumerate((bq, bk, bv))]
            loads += [(gates[:, 0:1], g_xattn.rearrange("(a o) -> a o", o=1).broadcast_to([P, 1])),
                      (gates[:, 1:2], g_ffn.rearrange("(a o) -> a o", o=1).broadcast_to([P, 1])),
                      (row_b[:, 0, :], bo.rearrange("(a d) -> a d", a=1).broadcast_to([P, D])),
                      (row_b[:, 1, :], b2.rearrange("(a d) -> a d", a=1).broadcast_to([P, D])),
                      (mask_u8[MROW:MROW + 1, :], mask_row),
                      (u1_sb[:, :, :], U1.rearrange("(j p) r -> p j r", p=P)),
                      (v1_sb[:, :], V1),
                      (u2_sb[:, :, :], U2.rearrange("(f p) r -> p f r", p=P)),
                      (v2_sb[0:RANK, :], V2), (v2_sb[RANK:P, :], V2),
                      (b1_col[:, :], b1.rearrange("(f p) -> p f", p=P))]
            assert 16 * len(loads) == CONST_LOADS
            with nc.allow_non_contiguous_dma(reason="columns of a few numbers"):
                for dst, src in loads:
                    act.dma_start(dst, src).then_inc(consts_in, 16)
            act.wait_ge(consts_in, CONST_LOADS)
            nc.scalar.activation(gates[:, :], gates[:, :], ACT.Tanh).then_inc(gates_done, 1)
            act.wait_ge(made_consts, 1)

            def project(i, last):
                for u in range(2):
                    b = 2 * i + u
                    act.wait_ge(ctx_turned, b + 1)
                    nc.scalar.activation(cT[:, :, :], ps[:, 0:2, :], ACT.Identity).then_inc(ctx_copied, 1)
                    act.wait_ge(v_done, b + 1)
                    nc.scalar.activation(v_all[:, :, bass.ds(TT * b, TT), :].rearrange("p h t d -> p t h d"),
                                         ps[:, 0:2, :].rearrange("p k (t h d) -> p (k t) h d", t=2, h=H),
                                         ACT.Identity).then_inc(v_copied, 1)
                    for z, bank, done, copied, scale in ((1, 4, k_done, k_copied, 1.0), (0, 6, q_done, q_copied, SCALE)):
                        act.wait_ge(done, b + 1)
                        act.wait_ge(split_done[z], b + 1)
                        act.wait_ge(parts_stored[z][u], 16 * (i + 1))
                        for j in range(J):
                            bias = qkv_b[:, z, j:j + 1]
                            nc.scalar.activation(parts[:, z, u, j, :], ps[:, bank + j, :], ACT.Identity, bias=bias, scale=scale)
                            ins = nc.scalar.activation(zf[:, z, j, :], ps[:, bank + j, :], ACT.Identity, bias=bias, scale=scale)
                        ins.then_inc(copied, 1)

            turns(act, B // 2, project)
            act.drain().then_inc(phase_end, 1)
            act.wait_ge(phase_end, BARRIER)

            def exponentials(i, s):
                for p in range(2):
                    act.wait_ge(turned, 2 * (SLOTS * i + s) + p + 1 + T_FREE)
                    if p == 0:
                        act.wait_ge(pv_done, 4 * i + s // GROUP + PV_FREE - 1)
                    nc.scalar.activation(p_sb[:, s % B, 2 * p:2 * p + 2, :], ps[:, 2 + 2 * p:4 + 2 * p, :], ACT.Exp).then_inc(exp_done, 1)

            exponentials(0, 0)

            def attend(i, last):
                for s in range(SLOTS):
                    if not (last and s + 1 == SLOTS):
                        exponentials(i, s + 1)
                    if s % GROUP == GROUP - 1:
                        h, half = s // B, s // GROUP % 2
                        act.wait_ge(pv_done, 4 * i + s // GROUP + 1 + PV_FREE)
                        act.wait_ge(o_stored[half], O_STORES * (2 * i + h + 1))
                        nc.scalar.activation(o_sb[:, half, :], ps[:, 6 + half, :], ACT.Identity).then_inc(o_copied, 1)

            turns(act, TURNS, attend)
            act.drain().then_inc(phase_end, 1)
            act.wait_ge(phase_end, 2 * BARRIER)

            def narrow(b):
                act.wait_ge(xn3_turned, b + 1)
                nc.scalar.activation(xnT[:, :, :], ps[:, 2:4, :], ACT.Identity).then_inc(xnT_copied, 1)
                act.wait_ge(rank_done, b + 1)
                nc.scalar.activation(pT[0:RANK, :], ps[0:RANK, 6, :], ACT.Identity).then_inc(rank_copied, 1)

            narrow(0)

            def finish(i, last):
                for u in range(2):
                    b = 2 * i + u
                    for f in range(FJ):
                        act.wait_ge(ff_done, FJ * b + f + 1)
                        nc.scalar.activation(hT[:, f, :], ps[:, 4 + f % 2, :], ACT.Gelu_apprx_tanh, bias=b1_col[:, f:f + 1]).then_inc(gelu_done, 1)
                    act.wait_ge(down_done, b + 1)
                    nc.scalar.activation(rT[:, :], ps[:, 7, :], ACT.Identity).then_inc(down_copied, 1)
                    if not (last and u == 1):
                        narrow(b + 1)

            turns(act, B // 2, finish)

        @block.vector
        def _(dve):
            nc.vector.memset(q_st[MROW:MROW + 1, :, :], 1.0)
            dve.wait_ge(consts_in, CONST_LOADS)
            nc.vector.tensor_scalar(qkv_b[:, 0, :], qkv_b[:, 0, :], SCALE, None, ALU.mult).then_inc(made_consts, 1)
            dve.wait_ge(gates_done, 1)
            nc.vector.tensor_scalar(row_b[:, 0, :], row_b[:, 0, :], gates[:, 0:1], None, ALU.mult)
            nc.vector.tensor_scalar(row_b[:, 1, :], row_b[:, 1, :], gates[:, 1:2], None, ALU.mult).then_inc(made_consts, 1)
            for w in range(4):
                dve.wait_ge(wt_done, w + 1)
                nc.vector.tensor_copy(wT[:, w].rearrange("p j d -> p (j d)"), ps[:, w, :]).then_inc(wt_copied, 1)

            def statistics(b, i, u, src, ready, want, stats_done, done):
                dve.wait_ge(ready, want)
                for t in range(TT):
                    ins = nc.vector.bn_stats(stats[:, t, :], src[:, u, t, :])
                ins.then_inc(stats_done, 1)
                dve.wait_ge(stats_done, b + 1)
                dve.sem_inc(passed_dve, 1)
                for t in range(TT):
                    ins = nc.vector.bn_aggr(mv[:, t, :], stats[:, t, :])
                ins.then_inc(done, 1)

            def normalise(b, dst, src, root_done, done):
                dve.wait_ge(root_done, b + 1)
                for t in range(TT):
                    ins = nc.vector.tensor_scalar(dst[:, t, :], src[:, t, :], mv[:, t, 0:1], rstd[:, t:t + 1], ALU.subtract, ALU.mult)
                ins.then_inc(done, 1)

            def split(z, b, u, n, copied):
                dve.wait_ge(copied, b + 2)
                nc.vector.tensor_tensor(zf[:, z], zf[:, z], parts[:, z, u, 0:J, :], ALU.subtract).then_inc(rest_done, 1)
                dve.wait_ge(rest_done, n)
                nc.vector.tensor_copy(parts[:, z, u, J:2 * J, :], zf[:, z]).then_inc(middle_done, 1)
                dve.wait_ge(middle_done, n)
                nc.vector.tensor_tensor(parts[:, z, u, 2 * J:3 * J, :], zf[:, z], parts[:, z, u, J:2 * J, :], ALU.subtract).then_inc(split_done[z], 1)

            statistics(0, 0, 0, x_in, x_loaded[0], 16, half_stats, moments)
            normalise(0, x_in[:, 0], x_in[:, 0], rstd_done, xn_done)

            def project(i, last):
                for u in range(2):
                    b, v = 2 * i + u, 1 - u
                    dve.wait_ge(x_turned, b + 1)
                    nc.vector.tensor_copy(xT[:, :, :], ps[:, 2:4, :]).then_inc(x_copied, 1)
                    more = not (last and u == 1)
                    if more:
                        statistics(b + 1, i, v, x_in, x_loaded[v], 16 * (i + u + 1), half_stats, moments)
                    split(1, b, u, 2 * b + 1, k_copied)
                    if more:
                        normalise(b + 1, x_in[:, v], x_in[:, v], rstd_done, xn_done)
                    split(0, b, u, 2 * b + 2, q_copied)

            turns(dve, B // 2, project)
            nc.vector.tensor_scalar(k_st[MROW:MROW + 1, 0, :], mask_u8[MROW:MROW + 1, :], MASKED, -MASKED, ALU.mult, ALU.add).then_inc(mask_done, 1)
            dve.wait_ge(mask_done, 1)
            nc.vector.tensor_copy(k_st[MROW:MROW + 1, 1, :], k_st[MROW:MROW + 1, 0, :])
            dve.drain().then_inc(phase_end, 1)
            dve.wait_ge(phase_end, BARRIER)

            def attend(i, last):
                for s in range(SLOTS):
                    u, w, g = s // B, s % 2, SLOTS * i + s
                    if s % B == 0:
                        dve.wait_ge(bias_in[u], 16 * (i + 1))
                    dve.wait_ge(turned, 2 * g + 2)
                    for t in range(TT):
                        dve.wait_ge(scores_done, TT * g + t + 1)
                        dve.sem_inc(passed_dve, 1)
                        nc.vector.tensor_tensor_reduce(out=t_sb[:, w, t, :], in0=ps[:, t % 2, :], in1=bias_sb[:, u, t, :], scale=1.0,
                                                       scalar=LOWEST, op0=ALU.add, op1=ALU.max, accum_out=mx[:, w, t:t + 1]).then_inc(biased, 1)
                    dve.wait_ge(biased, TT * g + 1)
                    nc.vector.tensor_scalar(t_sb[:, w, 0, :], t_sb[:, w, 0, :], mx[:, w, 0:1], None, ALU.subtract).then_inc(lowered_dve, 1)

            turns(dve, TURNS, attend)
            dve.drain().then_inc(phase_end, 1)
            dve.wait_ge(phase_end, 2 * BARRIER)

            dve.wait_ge(dens_in, 16)
            nc.vector.reciprocal(dens, dens).then_inc(recip_done, 1)

            def scale_values(b, i, u):
                dve.wait_ge(n_loaded[u], BATCH_LOADS * (i + 1))
                nc.vector.tensor_tensor(n_in[:, u], n_in[:, u], r_in[:, u], ALU.mult).then_inc(o_scaled, 1)

            def residual(b, i, u):
                dve.wait_ge(proj_done, b + 1)
                dve.wait_ge(x_biased, b + 1)
                nc.vector.scalar_tensor_tensor(out=x1[:, u].rearrange("p t d -> p (t d)"), in0=ps[:, 0:2, :].rearrange("p k s -> p (k s)"),
                                               scalar=gates[:, 0:1], in1=x3[:, u].rearrange("p t d -> p (t d)"),
                                               op0=ALU.mult, op1=ALU.add).then_inc(x1_done, 1)
                statistics(b, i, u, x1, x1_done, b + 1, half_stats3, moments3)

            scale_values(0, 0, 0)
            scale_values(1, 0, 1)
            residual(0, 0, 0)
            normalise(0, xn3, x1[:, 0], rstd3, xn3_done)

            def finish(i, last):
                for u in range(2):
                    b, v = 2 * i + u, 1 - u
                    if not (last and u == 1):
                        residual(b + 1, i + u, v)
                        dve.wait_ge(xn3_turned, b + 1)
                        normalise(b + 1, xn3, x1[:, v], rstd3, xn3_done)
                    if not last:
                        scale_values(b + 2, i + 1, u)
                    dve.wait_ge(ffn_done, b + 1)
                    dve.wait_ge(x1_biased, b + 1)
                    dve.wait_ge(y_stored[u], 16 * (i + 1))
                    nc.vector.scalar_tensor_tensor(out=y_out[:, u], in0=ps[:, 0:2, :].rearrange("p k (t d) -> p (k t) d", t=2),
                                                   scalar=gates[:, 1:2], in1=x1[:, u], op0=ALU.mult, op1=ALU.add).then_inc(y_done, 1)

            turns(dve, B // 2, finish)

        @block.tensor
        def _(pe):
            pe.wait_ge(ident_done, 1)
            pe.wait_ge(weights_in, 64)
            for w in range(4):
                for jo in range(J):
                    for ji in range(J):
                        lo = ji * D + jo * P
                        ins = nc.tensor.transpose(ps[:, w, lo:lo + P], w_raw[:, w, jo, ji * P:(ji + 1) * P], ident[:, :])
                ins.then_inc(wt_done, 1)
            pe.wait_ge(wt_copied, 4)

            def turn_tokens(src, bank):
                for j in range(J):
                    for t in range(TT):
                        ins = nc.tensor.transpose(ps[:, bank + j, t * P:(t + 1) * P], src[:, t, j * P:(j + 1) * P], ident[:, :])
                return ins

            def by_tokens(bank, lhsT, rhs):
                for t in range(TT):
                    dst = ps[:, bank + t // 2, (t % 2) * D:(t % 2 + 1) * D]
                    for n, (a, c) in enumerate(zip(lhsT(t), rhs)):
                        ins = nc.tensor.matmul(dst, a, c, start=(n == 0), stop=(n == len(rhs) - 1))
                return ins

            def by_width(bank, w, src):
                for jo in range(J):
                    for ji in range(J):
                        ins = nc.tensor.matmul(ps[:, bank + jo, :], wT[:, w, ji, jo * P:(jo + 1) * P], src[:, ji, :],
                                               start=(ji == 0), stop=(ji == J - 1))
                return ins

            def project(i, last):
                for u in range(2):
                    b = 2 * i + u
                    pe.wait_ge(c_loaded[u], 16 * (i + 1))
                    pe.wait_ge(v_copied, b + 1)
                    turn_tokens(c_in[:, u], 0).then_inc(ctx_turned, 1)
                    pe.wait_ge(xn_done, b + 1)
                    pe.wait_ge(x_copied, b + 1)
                    turn_tokens(x_in[:, u], 2).then_inc(x_turned, 1)
                    pe.wait_ge(ctx_copied, b + 1)
                    by_tokens(0, lambda t: [cT[:, j, t * P:(t + 1) * P] for j in range(J)], [wT[:, 2, j, :] for j in range(J)]).then_inc(v_done, 1)
                    pe.wait_ge(k_copied, b + 1)
                    by_width(4, 1, cT).then_inc(k_done, 1)
                    pe.wait_ge(x_copied, b + 2)
                    pe.wait_ge(q_copied, b + 1)
                    by_width(6, 0, xT).then_inc(q_done, 1)

            turns(pe, B // 2, project)
            pe.drain().then_inc(phase_end, 1)
            pe.wait_ge(phase_end, BARRIER)

            def scores(i, s, free=True):
                u, b, n = s // B % 2, s % B, TT * (SLOTS * i + s)
                if s % B == 0:
                    pe.wait_ge(stack_in[u], STACKS * (i + s // SLOTS + 1))
                for t in range(TT):
                    if free or n + t >= 2:
                        pe.wait_ge(biased, n + t - 1)
                    lo = b * S + t * P
                    nc.tensor.matmul(ps[:, t % 2, :], q_st[0:MROW + 1, u, lo:lo + P], k_st[0:MROW + 1, u, b * S:(b + 1) * S],
                                     start=True, stop=True).then_inc(scores_done, 1)

            def turn_scores(i, s, free=True):
                w, g = s % 2, SLOTS * i + s
                pe.wait_ge(lowered_pool, g + 1)
                pe.wait_ge(lowered_dve, g + 1)
                for p in range(2):
                    if free:
                        pe.wait_ge(exp_done, 2 * g + p - 1)
                    for k in range(2 * p, 2 * p + 2):
                        for t in range(TT):
                            ins = nc.tensor.transpose(ps[:, 2 + k, t * P:(t + 1) * P], t_sb[:, w, t, k * P:(k + 1) * P], ident[:, :])
                    ins.then_inc(turned, 1)

            def values(i, s):
                h, half, k = s // B, s // GROUP % 2, 4 * i + s // GROUP
                pe.wait_ge(exp_done, 2 * GROUP * (k + 1))
                pe.wait_ge(v_window, 2 * i + h + 1)
                pe.wait_ge(o_copied, k + 1)
                for t in range(TT):
                    for g in range(GROUP):
                        b = GROUP * half + g
                        ins = nc.tensor.matmul(ps[VW * g:VW * (g + 1), 6 + half, :], v_win[:, h, b * TT + t, :], p_sb[:, b, t, :],
                                               start=(t == 0), stop=(t == TT - 1))
                ins.then_inc(pv_done, 1)

            scores(0, 0, free=False)
            scores(0, 1)
            turn_scores(0, 0, free=False)

            def attend(i, last):
                for s in range(SLOTS):
                    if not (last and s + 2 >= SLOTS):
                        scores(i, s + 2)
                    if not (last and s + 1 >= SLOTS):
                        turn_scores(i, s + 1)
                    if s % GROUP == GROUP - 1:
                        values(i, s)

            turns(pe, TURNS, attend)
            pe.drain().then_inc(phase_end, 1)
            pe.wait_ge(phase_end, 2 * BARRIER)

            def project_out(b, u):
                pe.wait_ge(o_ready, b + 1)
                by_tokens(0, lambda t: [n_in[:, u, j, t * P:(t + 1) * P] for j in range(J)], [wT[:, 3, j, :] for j in range(J)]).then_inc(proj_done, 1)

            def narrow(b):
                pe.wait_ge(xn3_done, b + 1)
                turn_tokens(xn3, 2).then_inc(xn3_turned, 1)
                pe.wait_ge(xnT_copied, b + 1)
                for j in range(J):
                    ins = nc.tensor.matmul(ps[0:RANK, 6, :], u1_sb[:, j, :], xnT[:, j, :], start=(j == 0), stop=(j == J - 1))
                ins.then_inc(rank_done, 1)

            def down(b, f):
                pe.wait_ge(gelu_done, FJ * b + f + 3)
                lo = RANK * (f % 2)
                return nc.tensor.matmul(ps[lo:lo + RANK, 7, :], u2_sb[:, f, :], hT[:, f, :], start=(f < 2), stop=(f >= FJ - 2))

            project_out(0, 0)
            narrow(0)

            def finish(i, last):
                for u in range(2):
                    b, v = 2 * i + u, 1 - u
                    if not (last and u == 1):
                        pe.wait_ge(x1_done, b + 1)
                        pe.wait_ge(y_done, b + 1)
                        project_out(b + 1, v)
                    pe.wait_ge(rank_copied, b + 1)
                    pe.wait_ge(down_copied, b + 1)
                    for f in range(FJ):
                        pe.wait_ge(gelu_done, FJ * b + f + 1)
                        nc.tensor.matmul(ps[:, 4 + f % 2, :], v1_sb[:, f * P:(f + 1) * P], pT[0:RANK, :], start=True, stop=True).then_inc(ff_done, 1)
                        if f:
                            down(b, f - 1)
                    down(b, FJ - 1).then_inc(down_done, 1)
                    pe.wait_ge(down_copied, b + 2)
                    if last and u == 1:
                        pe.wait_ge(y_done, b + 1)
                    else:
                        pe.wait_ge(x1_done, b + 2)
                    by_tokens(0, lambda t: [rT[:, t * P:(t + 1) * P]], [v2_sb[:, :]]).then_inc(ffn_done, 1)
                    if not (last and u == 1):
                        narrow(b + 1)

            turns(pe, B // 2, finish)


_INS = ['x', 'ctx_1024', 'mask_BxS2_bk1', 'g_xattn', 'g_ffn', 'L0_xattn_relative_bias', 'L0_xattn_Wq', 'L0_xattn_bq',
        'L0_xattn_Wk', 'L0_xattn_bk', 'L0_xattn_Wv', 'L0_xattn_bv', 'L0_xattn_Wo', 'L0_xattn_bo',
        'L0_ffn_U1', 'L0_ffn_V1', 'L0_ffn_b1', 'L0_ffn_U2', 'L0_ffn_V2', 'L0_ffn_b2']


def kernel(**inputs):
    import numpy as _np
    import concourse.bacc as _bacc
    from concourse import mybir as _mybir
    from concourse.bass_utils import run_bass_kernel_spmd as _run

    nc = _bacc.Bacc("TRN2", target_bir_lowering=False, num_devices=1)
    arrays, args = {}, {}
    for name in _INS:
        a = _np.ascontiguousarray(inputs[name])
        arrays[f"in_{name}_dram"] = a
        args[name] = nc.dram_tensor(f"in_{name}_dram", a.shape, _mybir.dt.from_np(a.dtype), kind="ExternalInput").ap()
    out = nc.dram_tensor("out_0_dram", (B, S, D), F32, kind="ExternalOutput").ap()
    qk_parts = nc.dram_tensor("qk_parts_dram", (2, 3, D, B * S), BF16, kind="Internal").ap()
    values_raw = nc.dram_tensor("values_raw_dram", (B, D, S), F32, kind="Internal").ap()
    sums = nc.dram_tensor("sums_dram", (B, H, S), F32, kind="Internal").ap()
    recips = nc.dram_tensor("recips_dram", (B, H, S), F32, kind="Internal").ap()
    flamingo_kernel(nc, *[args[n] for n in _INS], out, qk_parts, values_raw, sums, recips)
    r = _run(nc, [arrays], core_ids=[0])
    return r.results[0]["out_0_dram"]
```

```python
from contextlib import ExitStack

import concourse.bass as bass
from concourse import mybir

F32 = mybir.dt.float32
F32R = mybir.dt.float32r
BF16 = mybir.dt.bfloat16
U8 = mybir.dt.uint8
ALU = mybir.AluOpType
ACT = mybir.ActivationFunctionType

P = 128
B, S, D = 8, 512, 256
H, DH = 16, 16
J = D // P
TT = S // P
FF, RANK = 1024, 64
FJ = FF // P
HPJ = P // DH
TERMS = 6
ROWS = TERMS * DH
QUERY_PARTS = [(0, 3), (1, 2), (2, 1)]
KEY_PARTS = [(0, 3), (0, 2), (0, 1)]
MASKED = 1.0e30
LOWEST = -3.0e38
EPS = 1.0e-5
SCALE = DH ** -0.5
GROUP = 4
VW = 32
SLOTS = 2 * B
TURNS = H // 2
AHEAD_T = GROUP
AHEAD_S = AHEAD_T + 1
EARLY = B - 2
MROW = ROWS

PV_FREE = 1
T_FREE = 4
O_STORES = 16 * GROUP
STACKS = 16 * (len(QUERY_PARTS) + len(KEY_PARTS))
BATCH_LOADS = 16 * 2
N_CONSTS = 13


def flamingo_kernel(nc, x, ctx_in, mask, g_xattn, g_ffn, rel_bias, Wq, bq, Wk, bk, Wv, bv, Wo, bo,
                    U1, V1, b1, U2, V2, b2, out, qk_parts, values):
    with ExitStack() as ctx:
        def sb(name, shape, dt=F32, stack=ctx):
            return stack.enter_context(nc.sbuf_tensor(name, shape, dt))

        def sem(name):
            return ctx.enter_context(nc.semaphore(name))

        ps = ctx.enter_context(nc.psum_tensor("ps", [P, 8, 512], F32))

        ident = sb("ident", [P, P])
        wT_h = sb("wT_h", [P, 4, J, D], F32R)
        wT_l = sb("wT_l", [P, 4, J, D], F32R)
        u1_h = sb("u1_h", [P, J, 2 * RANK], F32R)
        u1_l = sb("u1_l", [P, J, 2 * RANK], F32R)
        v1_h = sb("v1_h", [P, FF], F32R)
        v1_l = sb("v1_l", [P, FF], F32R)
        u2_sb = sb("u2_sb", [P, FJ, RANK])
        v2_sb = sb("v2_sb", [P, D])
        b1_col = sb("b1_col", [P, FJ])
        qk_b = sb("qk_b", [P, 2, J])
        bv_row = sb("bv_row", [P, D])
        row_b = sb("row_b", [P, 2, D])
        gates = sb("gates", [P, 2])
        eps4 = sb("eps4", [P, 2, TT])
        stats = sb("stats", [P, TT, 6])
        mv = sb("mv", [P, TT, 2])
        rstd = sb("rstd", [P, TT])

        v_all = sb("v_all", [P, H, B * TT, DH])
        bias_sb = sb("bias_sb", [P, 2, TT, S])
        q_st = sb("q_st", [P, 2, B * S], BF16)
        k_st = sb("k_st", [P, 2, B * S], BF16)
        v_win = sb("v_win", [P, 2, B * TT, VW])
        o_sb = sb("o_sb", [P, 2, S])
        o_turned = sb("o_turned", [P, S // VW, VW])
        o_recip = sb("o_recip", [P, S // VW])
        mx = sb("mx", [P, 2, TT])
        mask_u8 = o_sb[:, :, :].rearrange("p u s -> p (u s)").bitcast(U8)

        with ExitStack() as phase:
            x_in = sb("x_in", [P, 2, TT, D], stack=phase)
            c_in = sb("c_in", [P, 2, TT, D], stack=phase)
            xT_h = sb("xT_h", [P, J, S], F32R, stack=phase)
            xT_l = sb("xT_l", [P, J, S], F32R, stack=phase)
            cT_h = sb("cT_h", [P, J, S], F32R, stack=phase)
            cT_l = sb("cT_l", [P, J, S], F32R, stack=phase)
            zf = sb("zf", [P, 2, J, S], stack=phase)
            parts = sb("parts", [P, 2, 2, 3 * J, S], BF16, stack=phase)
            w_raw = sb("w_raw", [P, 4, J, D], stack=phase)
            v1_raw = sb("v1_raw", [P, FF], stack=phase)
            u1_raw = sb("u1_raw", [P, J, 2 * RANK], stack=phase)
        with ExitStack() as phase:
            p_sb = sb("p_sb", [P, B, TT, S], stack=phase)
            t_sb = sb("t_sb", [P, 2, TT, S], stack=phase)
        with ExitStack() as phase:
            n_in = sb("n_in", [P, 2, J, S], stack=phase)
            n_h = sb("n_h", [P, J, S], F32R, stack=phase)
            n_l = sb("n_l", [P, J, S], F32R, stack=phase)
            x3 = sb("x3", [P, 2, TT, D], stack=phase)
            x1 = sb("x1", [P, 2, TT, D], stack=phase)
            xn3 = sb("xn3", [P, TT, D], stack=phase)
            xnT_h = sb("xnT_h", [P, J, S], F32R, stack=phase)
            xnT_l = sb("xnT_l", [P, J, S], F32R, stack=phase)
            pT = sb("pT", [P, S], F32R, stack=phase)
            hT = sb("hT", [P, FJ, S], stack=phase)
            rT = sb("rT", [P, S], stack=phase)
            y_out = sb("y_out", [P, 2, TT, D], stack=phase)

        passed_sp = sem("passed_sp")
        passed_dve = sem("passed_dve")
        ident_zero = sem("ident_zero")
        ident_done = sem("ident_done")
        win_zero = sem("win_zero")
        eps_done = sem("eps_done")
        weights_in = [sem(f"weights_in{w}") for w in range(4)]
        biases_in = sem("biases_in")
        consts_in = sem("consts_in")
        bq_scaled = sem("bq_scaled")
        gates_done = sem("gates_done")
        rows_done = sem("rows_done")
        wt_done = sem("wt_done")
        wt_high = sem("wt_high")
        wt_low = sem("wt_low")
        ffn_high = sem("ffn_high")
        mask_done = sem("mask_done")
        x_loaded = [sem(f"x_loaded{u}") for u in range(2)]
        c_loaded = [sem(f"c_loaded{u}") for u in range(2)]
        half_stats = sem("half_stats")
        moments = sem("moments")
        var_eps = sem("var_eps")
        rstd_done = sem("rstd_done")
        xn_done = sem("xn_done")
        ctx_turned = sem("ctx_turned")
        ctx_high = sem("ctx_high")
        ctx_low = sem("ctx_low")
        x_turned = sem("x_turned")
        x_high = sem("x_high")
        x_low = sem("x_low")
        v_done = sem("v_done")
        v_copied = sem("v_copied")
        qk_done = [sem("q_done"), sem("k_done")]
        qk_copied = [sem("q_copied"), sem("k_copied")]
        rest_done = [sem("q_rest"), sem("k_rest")]
        middle_done = [sem("q_middle"), sem("k_middle")]
        split_done = [sem("q_split"), sem("k_split")]
        parts_stored = [[sem(f"parts_stored{z}{u}") for u in range(2)] for z in range(2)]

        stack_early = sem("stack_early")
        stack_in = [sem(f"stack_in{u}") for u in range(2)]
        bias_in = [sem(f"bias_in{u}") for u in range(2)]
        scores_done = sem("scores_done")
        biased = sem("biased")
        lowered_pool = sem("lowered_pool")
        lowered_act = sem("lowered_act")
        turned = sem("turned")
        exp_done = sem("exp_done")
        v_window = sem("v_window")
        pv_done = sem("pv_done")
        o_read = sem("o_read")
        recip_done = sem("recip_done")
        o_scaled = sem("o_scaled")
        o_ready = sem("o_ready")
        o_stored = [sem(f"o_stored{u}") for u in range(2)]

        n_loaded = [sem(f"n_loaded{u}") for u in range(2)]
        n_high = sem("n_high")
        n_low = sem("n_low")
        x_biased = sem("x_biased")
        proj_done = sem("proj_done")
        x1_done = sem("x1_done")
        half_stats3 = sem("half_stats3")
        moments3 = sem("moments3")
        var_eps3 = sem("var_eps3")
        rstd3 = sem("rstd3")
        xn3_done = sem("xn3_done")
        xn3_turned = sem("xn3_turned")
        xnT_high = sem("xnT_high")
        xnT_low = sem("xnT_low")
        rank_done = sem("rank_done")
        rank_high = sem("rank_high")
        rank_low = sem("rank_low")
        ff_done = sem("ff_done")
        gelu_done = sem("gelu_done")
        down_done = sem("down_done")
        down_copied = sem("down_copied")
        ffn_done = sem("ffn_done")
        x1_biased = sem("x1_biased")
        y_done = sem("y_done")
        y_stored = [sem(f"y_stored{u}") for u in range(2)]

        mask_row = mask.rearrange("b s -> (b s)").rearrange("(a s) -> a s", a=1)
        x_v = x.rearrange("b (t p) d -> b p t d", p=P)
        c_v = ctx_in.rearrange("b (t p) d -> b p t d", p=P)
        out_v = out.rearrange("b (t p) d -> b p t d", p=P)
        bias_v = rel_bias.rearrange("o h (t p) k -> (o h) p t k", p=P)
        parts_v = qk_parts.rearrange("z k (j p) s -> z p (k j) s", p=P)
        values_v = values.rearrange("b (j p) s -> b p j s", p=P)

        def turns(eng, n, body):
            with eng.Fori(0, n - 1) as i:
                body(i, False)
            body(n - 1, True)

        block = ctx.enter_context(nc.Block())

        @block.sync
        def _(sp):
            def load_tokens(b, u):
                sp.dma_start(c_in[:, u], c_v[bass.ds(b, 1)].rearrange("o p t d -> (o p) t d")).then_inc(c_loaded[u], 16)
                sp.dma_start(x_in[:, u], x_v[bass.ds(b, 1)].rearrange("o p t d -> (o p) t d")).then_inc(x_loaded[u], 16)

            def load_bias(h, u):
                sp.dma_start(bias_sb[:, u], bias_v[bass.ds(h, 1)].rearrange("o p t k -> (o p) t k")).then_inc(bias_in[u], 16)

            def load_stacks(h, u, lo, hi, loaded):
                rows, cols = bass.ds(h * DH, DH), slice(lo * S, hi * S)
                row = 0
                for part, times in QUERY_PARTS:
                    src = qk_parts[0, part:part + 1, rows, cols].broadcast_to([times, DH, (hi - lo) * S])
                    sp.dma_start(q_st[row:row + times * DH, u, cols], src).then_inc(loaded, 16)
                    row += times * DH
                row = 0
                for part, n in KEY_PARTS:
                    sp.dma_start(k_st[row:row + n * DH, u, cols], qk_parts[1, part:part + n, rows, cols]).then_inc(loaded, 16)
                    row += n * DH

            load_tokens(0, 0)
            for w, src in ((2, Wv), (1, Wk), (0, Wq)):
                sp.dma_start(w_raw[:, w], src.rearrange("(j p) d -> p j d", p=P)).then_inc(weights_in[w], 16)
            load_tokens(1, 1)
            sp.dma_start(w_raw[:, 3], Wo.rearrange("(j p) d -> p j d", p=P)).then_inc(weights_in[3], 16)
            load_bias(0, 0)
            load_bias(1, 1)

            def project(i, last):
                if last:
                    for z in range(2):
                        for u in range(2):
                            sp.wait_ge(parts_stored[z][u], 16 + 16 * (EARLY // 2))
                    load_stacks(0, 0, 0, EARLY, stack_early)
                for u in range(2):
                    b = 2 * i + u
                    if not last:
                        sp.wait_ge(ctx_turned, b + 1)
                        sp.wait_ge(x_turned, b + 1)
                        sp.sem_inc(passed_sp, 1)
                        load_tokens(b + 2, u)
                    for z in (1, 0):
                        sp.wait_ge(split_done[z], b + 2)
                        sp.sem_inc(passed_sp, 1)
                        sp.dma_start(parts_v[z][:, :, bass.ds(b * S, S)], parts[:, z, u]).then_inc(parts_stored[z][u], 16)

            turns(sp, B // 2, project)
            for z in range(2):
                for u in range(2):
                    sp.wait_ge(parts_stored[z][u], 16 + 16 * (B // 2))
            load_stacks(0, 0, EARLY, B, stack_in[0])
            load_stacks(1, 1, 0, B, stack_in[1])

            def attend(i, last):
                for u in range(2):
                    if not last:
                        sp.wait_ge(biased, TT * B * (2 * i + u + 1))
                        sp.sem_inc(passed_sp, 1)
                        load_bias(2 * i + u + 2, u)
                        load_stacks(2 * i + u + 2, u, 0, B, stack_in[u])
                    for half in range(2):
                        sp.wait_ge(o_ready, 4 * i + 2 * u + half + 1)
                        sp.sem_inc(passed_sp, 1)
                        for g in range(GROUP):
                            sp.dma_start(values[GROUP * half + g, bass.ds((2 * i + u) * DH, DH), :],
                                         o_sb[VW * g:VW * g + DH, half, :]).then_inc(o_stored[half], 16)
                        if last and u == 1:
                            sp.wait_ge(o_stored[half], O_STORES * (H + 1))
                            if half == 0:
                                sp.wait_ge(pv_done, PV_FREE + 2 * H - 1)
                                load_batch(0, 0)
                                load_batch(1, 1)

            def load_batch(b, u):
                sp.dma_start(n_in[:, u], values_v[bass.ds(b, 1)].rearrange("o p j s -> (o p) j s")).then_inc(n_loaded[u], 16)
                sp.dma_start(x3[:, u], x_v[bass.ds(b, 1)].rearrange("o p t d -> (o p) t d")).then_inc(n_loaded[u], 16)

            turns(sp, TURNS, attend)

            def finish(i, last):
                for u in range(2):
                    b = 2 * i + u
                    if not last:
                        sp.wait_ge(n_low, b + 1)
                        sp.wait_ge(x1_done, b + 1)
                        sp.sem_inc(passed_sp, 1)
                        load_batch(b + 2, u)
                    sp.wait_ge(y_done, b + 2)
                    sp.sem_inc(passed_sp, 1)
                    sp.dma_start(out_v[bass.ds(b, 1)].rearrange("o p t d -> (o p) t d"), y_out[:, u]).then_inc(y_stored[u], 16)

            turns(sp, B // 2, finish)
            for u in range(2):
                sp.wait_ge(y_stored[u], 16 * (B // 2 + 1))

        @block.gpsimd
        def _(pool):
            nc.gpsimd.memset(ident[:, :], 0.0).then_inc(ident_zero, 1)
            pool.wait_ge(ident_zero, 1)
            nc.gpsimd.affine_select(out=ident[:, :], in_=ident[:, :], compare_op=ALU.not_equal, fill=1.0, base=0,
                                    pattern=[[-1, P]], channel_multiplier=1).then_inc(ident_done, 1)
            for s in (*qk_copied, *split_done, down_copied, y_done):
                pool.sem_inc(s, 1)
            for s, n in ((o_read, 2), (turned, T_FREE), (pv_done, PV_FREE), (gelu_done, 2)):
                pool.sem_inc(s, n)
            for u in range(2):
                for z in range(2):
                    pool.sem_inc(parts_stored[z][u], 16)
                pool.sem_inc(o_stored[u], O_STORES)
                pool.sem_inc(y_stored[u], 16)
            nc.gpsimd.memset(eps4[:, 0, :], EPS)
            nc.gpsimd.memset(eps4[:, 1, :], -0.5).then_inc(eps_done, 1)
            pool.wait_ge(eps_done, 1)

            def reciprocal_root(b, ready, out_ap, var, done_eps, done):
                pool.wait_ge(ready, b + 1)
                nc.gpsimd.tensor_tensor(out_ap, var, eps4[:, 0, :], ALU.add).then_inc(done_eps, 1)
                pool.wait_ge(done_eps, b + 1)
                nc.gpsimd.tensor_tensor(out_ap, out_ap, eps4[:, 1, :], ALU.pow).then_inc(done, 1)

            def low_part(z, b, u):
                pool.wait_ge(middle_done[z], b + 1)
                nc.gpsimd.tensor_tensor(parts[:, z, u, 2 * J:3 * J, :], zf[:, z], parts[:, z, u, J:2 * J, :],
                                        ALU.subtract).then_inc(split_done[z], 1)

            reciprocal_root(0, moments, rstd[:, :], mv[:, :, 1], var_eps, rstd_done)
            for u in range(2):
                nc.gpsimd.memset(v_win[:, u], 0.0).then_inc(win_zero, 1)
            pool.wait_ge(win_zero, 2)
            nc.gpsimd.memset(v_win[:, :, :, DH:DH + 1], 1.0).then_inc(win_zero, 1)
            pool.wait_ge(win_zero, 3)

            def project(i, last):
                for u in range(2):
                    b = 2 * i + u
                    if not (last and u == 1):
                        reciprocal_root(b + 1, moments, rstd[:, :], mv[:, :, 1], var_eps, rstd_done)
                    low_part(1, b, u)
                    low_part(0, b, u)

            turns(pool, B // 2, project)

            def take_values(h, u):
                nc.gpsimd.tensor_copy(v_win[:, u, :, 0:DH], v_all[:, bass.ds(h, 1), :, :].rearrange("p o t d -> p (o t) d")).then_inc(v_window, 1)

            def lower(i, s):
                for t in range(2):
                    pool.wait_ge(biased, TT * (SLOTS * i + s) + t + 1)
                    ins = nc.gpsimd.tensor_tensor(t_sb[:, s % 2, t, :], mx[:, s % 2, t:t + 1].broadcast_to([P, S]),
                                                  t_sb[:, s % 2, t, :], ALU.subtract)
                ins.then_inc(lowered_pool, 1)

            pool.wait_ge(v_copied, B)
            take_values(0, 0)
            for s in range(AHEAD_S):
                lower(0, s)

            def attend(i, last):
                for s in range(SLOTS):
                    if s == 0:
                        pool.wait_ge(pv_done, 4 * i + PV_FREE)
                        take_values(2 * i + 1, 1)
                    if s == B and not last:
                        pool.wait_ge(pv_done, 4 * i + 2 + PV_FREE)
                        take_values(2 * i + 2, 0)
                    if not (last and s + AHEAD_S >= SLOTS):
                        lower(i, s + AHEAD_S)
                    if s % GROUP == GROUP - 1:
                        pool.wait_ge(recip_done, 4 * i + s // GROUP + 1)
                        nc.gpsimd.tensor_tensor(o_turned[:, :, 0:DH], o_turned[:, :, 0:DH],
                                                o_recip[:, :].rearrange("p (k o) -> p k o", o=1).broadcast_to([P, S // VW, DH]),
                                                ALU.mult).then_inc(o_scaled, 1)

            turns(pool, TURNS, attend)

            def bias_tokens(b, i, u):
                pool.wait_ge(n_loaded[u], BATCH_LOADS * (i + 1))
                row = row_b[:, 0:1, :].broadcast_to([P, TT, D])
                nc.gpsimd.tensor_tensor(x3[:, u], x3[:, u], row, ALU.add).then_inc(x_biased, 1)

            def after_attention(b, u):
                reciprocal_root(b, moments3, rstd[:, :], mv[:, :, 1], var_eps3, rstd3)
                pool.wait_ge(xn3_done, b + 1)
                row = row_b[:, 1:2, :].broadcast_to([P, TT, D])
                nc.gpsimd.tensor_tensor(x1[:, u], x1[:, u], row, ALU.add).then_inc(x1_biased, 1)

            pool.wait_ge(rows_done, 1)
            bias_tokens(0, 0, 0)
            after_attention(0, 0)

            def finish(i, last):
                for u in range(2):
                    if not (last and u == 1):
                        bias_tokens(2 * i + u + 1, i + u, 1 - u)
                        after_attention(2 * i + u + 1, 1 - u)

            turns(pool, B // 2, finish)

        @block.scalar
        def _(act):
            def column(v):
                return v.rearrange("(j p) -> p j", p=P)

            def row(v):
                return v.rearrange("(a d) -> a d", a=1).broadcast_to([P, D])

            def number(v):
                return v.rearrange("(a o) -> a o", o=1).broadcast_to([P, 1])

            def copy(dst, src):
                return nc.scalar.activation(dst, src, ACT.Identity)

            with nc.allow_non_contiguous_dma(reason="columns of a few numbers"):
                for dst, src in ((bv_row[:, :], row(bv)), (qk_b[:, 0, :], column(bq)), (qk_b[:, 1, :], column(bk))):
                    act.dma_start(dst, src).then_inc(biases_in, 16)

            def turn_high(w):
                act.wait_ge(wt_done, w + 1)
                n = (2, 1, 0, 3)[w]
                copy(wT_h[:, n].rearrange("p j d -> p (j d)"), ps[:, 4 + w, :]).then_inc(wt_high, 1)

            def ctx_parts(b):
                act.wait_ge(ctx_turned, b + 1)
                copy(cT_h[:, :, :], ps[:, 0:2, :]).then_inc(ctx_high, 1)

            def x_parts(b):
                act.wait_ge(x_turned, b + 1)
                copy(xT_h[:, :, :], ps[:, 2:4, :]).then_inc(x_high, 1)

            ctx_parts(0)
            for w in range(3):
                turn_high(w)
            x_parts(0)
            turn_high(3)
            act.wait_ge(bq_scaled, 1)

            def high_part(z, b, i, u):
                bank, scale = ((6, SCALE), (4, 1.0))[z]
                act.wait_ge(qk_done[z], b + 1)
                act.wait_ge(split_done[z], b + 1)
                act.wait_ge(parts_stored[z][u], 16 * (i + 1))
                for j in range(J):
                    bias = qk_b[:, z, j:j + 1]
                    nc.scalar.activation(parts[:, z, u, j, :], ps[:, bank + j, :], ACT.Identity, bias=bias, scale=scale)
                    ins = nc.scalar.activation(zf[:, z, j, :], ps[:, bank + j, :], ACT.Identity, bias=bias, scale=scale)
                ins.then_inc(qk_copied[z], 1)

            def middle_part(z, b, u):
                act.wait_ge(rest_done[z], b + 1)
                copy(parts[:, z, u, J:2 * J, :], zf[:, z]).then_inc(middle_done[z], 1)

            def project(i, last):
                for u in range(2):
                    b, more = 2 * i + u, not (last and u == 1)
                    if more:
                        ctx_parts(b + 1)
                    high_part(1, b, i, u)
                    if more:
                        x_parts(b + 1)
                    high_part(0, b, i, u)
                    middle_part(1, b, u)
                    middle_part(0, b, u)

            with nc.allow_non_contiguous_dma(reason="columns of a few numbers"):
                loads = [(u1_raw[:, :, 0:RANK], U1.rearrange("(j p) r -> p j r", p=P)),
                         (u1_raw[:, :, RANK:2 * RANK], U1.rearrange("(j p) r -> p j r", p=P)),
                         (v1_raw[0:RANK, :], V1), (v1_raw[RANK:P, :], V1),
                         (gates[:, 0:1], number(g_xattn)), (gates[:, 1:2], number(g_ffn)),
                         (row_b[:, 0, :], row(bo)), (row_b[:, 1, :], row(b2)),
                         (mask_u8[MROW:MROW + 1, :], mask_row),
                         (u2_sb[:, :, :], U2.rearrange("(f p) r -> p f r", p=P)),
                         (v2_sb[0:RANK, :], V2), (v2_sb[RANK:P, :], V2),
                         (b1_col[:, :], b1.rearrange("(f p) -> p f", p=P))]
                assert len(loads) == N_CONSTS
                for dst, src in loads:
                    act.dma_start(dst, src).then_inc(consts_in, 16)

            turns(act, B // 2, project)
            act.wait_ge(consts_in, 16 * N_CONSTS)
            copy(u1_h[:, :, :], u1_raw[:, :, :])
            copy(v1_h[:, :], v1_raw[:, :]).then_inc(ffn_high, 1)
            nc.scalar.activation(gates[:, :], gates[:, :], ACT.Tanh).then_inc(gates_done, 1)

            def lower(i, s):
                for t in range(2, TT):
                    act.wait_ge(biased, TT * (SLOTS * i + s) + t + 1)
                    ins = nc.scalar.activation(t_sb[:, s % 2, t, :], t_sb[:, s % 2, t, :], ACT.Identity, bias=mx[:, s % 2, t:t + 1], scale=-1.0)
                ins.then_inc(lowered_act, 1)

            def exponentials(i, s, p, free=True):
                act.wait_ge(turned, 2 * (SLOTS * i + s) + p + 1 + T_FREE)
                if free and p == 0:
                    act.wait_ge(pv_done, 4 * i + s // GROUP - 1 + PV_FREE)
                nc.scalar.activation(p_sb[:, s % B, 2 * p:2 * p + 2, :], ps[:, 2 + 2 * p:4 + 2 * p, :], ACT.Exp, scale=-1.0).then_inc(exp_done, 1)

            lower(0, 0)
            act.wait_ge(qk_done[0], B)
            for s in range(AHEAD_T):
                exponentials(0, s, 0, free=False)
                lower(0, s + 1)
                exponentials(0, s, 1, free=False)
            for z in range(2):
                act.wait_ge(split_done[z], B + 1)
                for u in range(2):
                    act.wait_ge(parts_stored[z][u], 16 * (B // 2 + 1))

            def attend(i, last):
                for s in range(SLOTS):
                    if not (last and s + AHEAD_T >= SLOTS):
                        exponentials(i, s + AHEAD_T, 0)
                    if not (last and s + AHEAD_S >= SLOTS):
                        lower(i, s + AHEAD_S)
                    if not (last and s + AHEAD_T >= SLOTS):
                        exponentials(i, s + AHEAD_T, 1)

            turns(act, TURNS, attend)

            def split_values(b, i, u):
                act.wait_ge(n_loaded[u], BATCH_LOADS * (i + 1))
                if not isinstance(b, int) or b:
                    act.wait_ge(proj_done, b)
                copy(n_h[:, :, :], n_in[:, u]).then_inc(n_high, 1)

            def narrow(b):
                act.wait_ge(xn3_turned, b + 1)
                copy(xnT_h[:, :, :], ps[:, 2:4, :]).then_inc(xnT_high, 1)
                act.wait_ge(rank_done, b + 1)
                copy(pT[:, :], ps[:, 6, :]).then_inc(rank_high, 1)

            split_values(0, 0, 0)
            act.wait_ge(pv_done, PV_FREE + 2 * H)
            narrow(0)
            split_values(1, 0, 1)

            def finish(i, last):
                for u in range(2):
                    b = 2 * i + u
                    for f in range(FJ):
                        act.wait_ge(ff_done, FJ * b + f + 1)
                        nc.scalar.activation(hT[:, f, :], ps[:, 4 + f % 2, :], ACT.Gelu_apprx_tanh, bias=b1_col[:, f:f + 1]).then_inc(gelu_done, 1)
                    act.wait_ge(down_done, b + 1)
                    copy(rT[:, :], ps[:, 7, :]).then_inc(down_copied, 1)
                    if not (last and u == 1):
                        narrow(b + 1)
                    if not last:
                        split_values(b + 2, i + 1, u)

            turns(act, B // 2, finish)

        @block.vector
        def _(dve):
            def less(dst, src, high):
                return nc.vector.tensor_tensor(dst, src, high.bitcast(F32), ALU.subtract)

            def statistics(b, src, ready, want, stats_done, done):
                dve.wait_ge(ready, want)
                for t in range(TT):
                    ins = nc.vector.bn_stats(stats[:, t, :], src[:, t, :])
                ins.then_inc(stats_done, 1)
                dve.wait_ge(stats_done, b + 1)
                dve.sem_inc(passed_dve, 1)
                for t in range(TT):
                    ins = nc.vector.bn_aggr(mv[:, t, :], stats[:, t, :])
                ins.then_inc(done, 1)

            def normalise(b, dst, src, root_done, done):
                dve.wait_ge(root_done, b + 1)
                for t in range(TT):
                    ins = nc.vector.tensor_scalar(dst[:, t, :], src[:, t, :], mv[:, t, 0:1], rstd[:, t:t + 1], ALU.subtract, ALU.mult)
                ins.then_inc(done, 1)

            def turn_low(w):
                dve.wait_ge(wt_high, w + 1)
                n = (2, 1, 0, 3)[w]
                less(wT_l[:, n].rearrange("p j d -> p (j d)"), ps[:, 4 + w, :], wT_h[:, n].rearrange("p j d -> p (j d)")).then_inc(wt_low, 1)

            def ctx_parts(b):
                dve.wait_ge(ctx_high, b + 1)
                less(cT_l[:, :, :], ps[:, 0:2, :], cT_h[:, :, :]).then_inc(ctx_low, 1)

            def x_parts(b):
                dve.wait_ge(x_high, b + 1)
                less(xT_l[:, :, :], ps[:, 2:4, :], xT_h[:, :, :]).then_inc(x_low, 1)

            def rest(z, b, u):
                dve.wait_ge(qk_copied[z], b + 2)
                nc.vector.tensor_tensor(zf[:, z], zf[:, z], parts[:, z, u, 0:J, :], ALU.subtract).then_inc(rest_done[z], 1)

            statistics(0, x_in[:, 0], x_loaded[0], 16, half_stats, moments)
            ctx_parts(0)
            normalise(0, x_in[:, 0], x_in[:, 0], rstd_done, xn_done)
            for w in range(3):
                turn_low(w)
            x_parts(0)
            turn_low(3)
            dve.wait_ge(biases_in, 48)
            nc.vector.tensor_scalar(qk_b[:, 0, :], qk_b[:, 0, :], SCALE, None, ALU.mult).then_inc(bq_scaled, 1)

            def project(i, last):
                for u in range(2):
                    b, v, more = 2 * i + u, 1 - u, not (last and u == 1)
                    dve.wait_ge(v_done, b + 1)
                    for k in range(2):
                        ins = nc.vector.tensor_tensor(v_all[:, :, bass.ds(TT * b + 2 * k, 2), :].rearrange("p h t d -> p t h d"),
                                                      ps[:, k, :].rearrange("p (t h d) -> p t h d", t=2, h=H),
                                                      bv_row[:, :].rearrange("p (o h d) -> p o h d", o=1, h=H).broadcast_to([P, 2, H, DH]),
                                                      ALU.add)
                    ins.then_inc(v_copied, 1)
                    if more:
                        statistics(b + 1, x_in[:, v], x_loaded[v], 16 * (i + u + 1), half_stats, moments)
                        normalise(b + 1, x_in[:, v], x_in[:, v], rstd_done, xn_done)
                        ctx_parts(b + 1)
                    rest(1, b, u)
                    if more:
                        x_parts(b + 1)
                    rest(0, b, u)

            turns(dve, B // 2, project)
            dve.wait_ge(consts_in, 16 * N_CONSTS)
            nc.vector.tensor_scalar(k_st[MROW:MROW + 1, 0, :], mask_u8[MROW:MROW + 1, :], MASKED, -MASKED, ALU.mult, ALU.add)
            nc.vector.tensor_scalar(q_st[MROW:MROW + 1, 0, :], mask_u8[MROW:MROW + 1, :], 0.0, 1.0, ALU.mult, ALU.add).then_inc(mask_done, 1)
            dve.wait_ge(mask_done, 1)
            nc.vector.tensor_copy(k_st[MROW:MROW + 1, 1, :], k_st[MROW:MROW + 1, 0, :])
            nc.vector.tensor_copy(q_st[MROW:MROW + 1, 1, :], q_st[MROW:MROW + 1, 0, :]).then_inc(mask_done, 1)
            dve.wait_ge(ffn_high, 1)
            less(u1_l[:, :, :], u1_raw[:, :, :], u1_h[:, :, :])
            less(v1_l[:, :], v1_raw[:, :], v1_h[:, :])
            dve.wait_ge(gates_done, 1)
            for n in range(2):
                ins = nc.vector.tensor_scalar(row_b[:, n, :], row_b[:, n, :], gates[:, n:n + 1], None, ALU.mult)
            ins.then_inc(rows_done, 1)

            def bias_scores(i, s, t, free=True):
                u, n = s // B % 2, TT * (SLOTS * i + s) + t
                if t == 0:
                    if s % B == 0:
                        dve.wait_ge(bias_in[u], 16 * (i + s // SLOTS + 1))
                    dve.wait_ge(turned, 2 * (SLOTS * i + s) + 2)
                dve.wait_ge(scores_done, n + 1)
                dve.sem_inc(passed_dve, 1)
                nc.vector.tensor_tensor_reduce(out=t_sb[:, s % 2, t, :], in0=ps[:, t % 2, :], in1=bias_sb[:, u, t, :], scale=1.0,
                                               scalar=LOWEST, op0=ALU.add, op1=ALU.max, accum_out=mx[:, s % 2, t:t + 1]).then_inc(biased, 1)

            for s in range(AHEAD_S):
                for t in range(TT):
                    bias_scores(0, s, t)

            def attend(i, last):
                for s in range(SLOTS):
                    k, half = 4 * i + s // GROUP, s // GROUP % 2
                    for t in range(TT):
                        if not (last and s + AHEAD_S >= SLOTS):
                            bias_scores(i, s + AHEAD_S, t)
                        if s % GROUP < GROUP - 1:
                            continue
                        if t == 0:
                            dve.wait_ge(pv_done, k + 1 + PV_FREE)
                            if last:
                                dve.wait_ge(o_ready, k)
                            nc.vector.transpose(o_turned[:, :, :].rearrange("p k c -> p (k c)"), ps[:, 6 + half, :]).then_inc(o_read, 1)
                        if t == 1:
                            dve.wait_ge(o_read, k + 3)
                            nc.vector.reciprocal(o_recip[:, :], o_turned[:, :, DH]).then_inc(recip_done, 1)
                        if t == 3:
                            dve.wait_ge(o_scaled, k + 1)
                            dve.wait_ge(o_stored[half], O_STORES * (2 * i + s // B + 1))
                            nc.vector.transpose(o_sb[:, half, :], o_turned[:, :, :].rearrange("p k c -> p (k c)")).then_inc(o_ready, 1)

            turns(dve, TURNS, attend)

            def split_values(b, u):
                dve.wait_ge(n_high, b + 1)
                less(n_l[:, :, :], n_in[:, u], n_h[:, :, :]).then_inc(n_low, 1)

            def residual(b, u):
                dve.wait_ge(proj_done, b + 1)
                dve.wait_ge(x_biased, b + 1)
                nc.vector.scalar_tensor_tensor(out=x1[:, u].rearrange("p t d -> p (t d)"), in0=ps[:, 0:2, :].rearrange("p k s -> p (k s)"),
                                               scalar=gates[:, 0:1], in1=x3[:, u].rearrange("p t d -> p (t d)"),
                                               op0=ALU.mult, op1=ALU.add).then_inc(x1_done, 1)

            def narrow(b):
                dve.wait_ge(xnT_high, b + 1)
                less(xnT_l[:, :, :], ps[:, 2:4, :], xnT_h[:, :, :]).then_inc(xnT_low, 1)
                dve.wait_ge(rank_high, b + 1)
                less(pT[RANK:P, :], ps[RANK:P, 6, :], pT[RANK:P, :]).then_inc(rank_low, 1)

            split_values(0, 0)
            residual(0, 0)
            statistics(0, x1[:, 0], x1_done, 1, half_stats3, moments3)
            dve.wait_ge(pv_done, PV_FREE + 2 * H)
            normalise(0, xn3, x1[:, 0], rstd3, xn3_done)
            narrow(0)
            split_values(1, 1)

            def finish(i, last):
                for u in range(2):
                    b, v, more = 2 * i + u, 1 - u, not (last and u == 1)
                    if more:
                        residual(b + 1, v)
                        statistics(b + 1, x1[:, v], x1_done, b + 2, half_stats3, moments3)
                        dve.wait_ge(xn3_turned, b + 1)
                        normalise(b + 1, xn3, x1[:, v], rstd3, xn3_done)
                    dve.wait_ge(ffn_done, b + 1)
                    dve.wait_ge(x1_biased, b + 1)
                    dve.wait_ge(y_stored[u], 16 * (i + 1))
                    nc.vector.scalar_tensor_tensor(out=y_out[:, u], in0=ps[:, 0:2, :].rearrange("p k (t d) -> p (k t) d", t=2),
                                                   scalar=gates[:, 1:2], in1=x1[:, u], op0=ALU.mult, op1=ALU.add).then_inc(y_done, 1)
                    if more:
                        narrow(b + 1)
                    if not last:
                        split_values(b + 2, u)

            turns(dve, B // 2, finish)

        @block.tensor
        def _(pe):
            def turn_weight(w):
                n = (2, 1, 0, 3)[w]
                pe.wait_ge(weights_in[n], 16)
                for jo in range(J):
                    for ji in range(J):
                        lo = ji * D + jo * P
                        ins = nc.tensor.transpose(ps[:, 4 + w, lo:lo + P], w_raw[:, n, jo, ji * P:(ji + 1) * P], ident[:, :])
                ins.then_inc(wt_done, 1)

            def turn_tokens(src, bank):
                for j in range(J):
                    for t in range(TT):
                        ins = nc.tensor.transpose(ps[:, bank + j, t * P:(t + 1) * P], src[:, t, j * P:(j + 1) * P], ident[:, :])
                return ins

            def three(pairs, dst):
                terms = [(a, b) for a_h, a_l, b_h, b_l in pairs for a, b in ((a_h, b_h), (a_h, b_l), (a_l, b_h))]
                for n, (a, b) in enumerate(terms):
                    ins = nc.tensor.matmul(dst, a, b, start=(n == 0), stop=(n == len(terms) - 1))
                return ins

            def by_tokens(bank, src_h, src_l, w):
                for t in range(TT):
                    cols = slice(t * P, (t + 1) * P)
                    ins = three([(src_h[:, j, cols], src_l[:, j, cols], wT_h[:, w, j, :], wT_l[:, w, j, :]) for j in range(J)],
                                ps[:, bank + t // 2, (t % 2) * D:(t % 2 + 1) * D])
                return ins

            def by_width(bank, w, src_h, src_l):
                for jo in range(J):
                    cols = slice(jo * P, (jo + 1) * P)
                    ins = three([(wT_h[:, w, j, cols], wT_l[:, w, j, cols], src_h[:, j, :], src_l[:, j, :]) for j in range(J)],
                                ps[:, bank + jo, :])
                return ins

            pe.wait_ge(ident_done, 1)
            pe.wait_ge(c_loaded[0], 16)
            turn_tokens(c_in[:, 0], 0).then_inc(ctx_turned, 1)
            for w in range(3):
                turn_weight(w)
            pe.wait_ge(xn_done, 1)
            turn_tokens(x_in[:, 0], 2).then_inc(x_turned, 1)
            turn_weight(3)
            pe.wait_ge(wt_low, 4)

            def project(i, last):
                for u in range(2):
                    b, v, more = 2 * i + u, 1 - u, not (last and u == 1)
                    pe.wait_ge(ctx_low, b + 1)
                    by_tokens(0, cT_h, cT_l, 2).then_inc(v_done, 1)
                    pe.wait_ge(qk_copied[1], b + 1)
                    by_width(4, 1, cT_h, cT_l).then_inc(qk_done[1], 1)
                    if more:
                        pe.wait_ge(c_loaded[v], 16 * (i + u + 1))
                        pe.wait_ge(v_copied, b + 1)
                        turn_tokens(c_in[:, v], 0).then_inc(ctx_turned, 1)
                    pe.wait_ge(x_low, b + 1)
                    pe.wait_ge(qk_copied[0], b + 1)
                    by_width(6, 0, xT_h, xT_l).then_inc(qk_done[0], 1)
                    if more:
                        pe.wait_ge(xn_done, b + 2)
                        turn_tokens(x_in[:, v], 2).then_inc(x_turned, 1)

            turns(pe, B // 2, project)

            def scores(i, s, t):
                u, b, n = s // B % 2, s % B, TT * (SLOTS * i + s) + t
                if s % B == 0 and t == 0 and s:
                    pe.wait_ge(stack_in[u], STACKS * (i + s // SLOTS + 1))
                if s or t >= 2:
                    pe.wait_ge(biased, n - 1)
                lo = b * S + t * P
                nc.tensor.matmul(ps[:, t % 2, :], q_st[0:MROW + 1, u, lo:lo + P], k_st[0:MROW + 1, u, b * S:(b + 1) * S],
                                 start=True, stop=True).then_inc(scores_done, 1)

            def turn_scores(i, s, k, free=True):
                w, g = s % 2, SLOTS * i + s
                if k == 0:
                    pe.wait_ge(lowered_pool, g + 1)
                    pe.wait_ge(lowered_act, g + 1)
                if k % 2 == 0 and free:
                    pe.wait_ge(exp_done, 2 * g + k // 2 - 1)
                for t in range(TT):
                    ins = nc.tensor.transpose(ps[:, 2 + k, t * P:(t + 1) * P], t_sb[:, w, t, k * P:(k + 1) * P], ident[:, :])
                if k % 2:
                    ins.then_inc(turned, 1)

            def weigh(i, s):
                h, half, k, t = s // B, s // GROUP % 2, 4 * i + s // GROUP, s % GROUP
                if t == 0:
                    pe.wait_ge(v_window, 2 * i + h + 1)
                    pe.wait_ge(o_read, k + 1)
                if t % 2 == 0:
                    pe.wait_ge(exp_done, 2 * GROUP * (k + 1) - 1 + t // 2)
                for g in range(GROUP):
                    b = GROUP * half + g
                    ins = nc.tensor.matmul(ps[VW * g:VW * (g + 1), 6 + half, :], v_win[:, h, b * TT + t, :], p_sb[:, b, t, :],
                                           start=(t == 0), stop=(t == TT - 1))
                if t == TT - 1:
                    ins.then_inc(pv_done, 1)

            pe.wait_ge(mask_done, 2)
            pe.wait_ge(v_copied, B)
            pe.wait_ge(stack_early, STACKS)
            for t in range(TT):
                scores(0, 0, t)
            pe.wait_ge(qk_copied[1], B + 1)
            for s in range(AHEAD_T):
                for t in range(TT):
                    scores(0, s + 1, t)
                    turn_scores(0, s, t, free=s > 0)
            pe.wait_ge(qk_copied[0], B + 1)
            pe.wait_ge(stack_in[0], STACKS)

            def attend(i, last):
                for s in range(SLOTS):
                    weigh(i, s)
                    for t in range(TT):
                        if not (last and s + AHEAD_S >= SLOTS):
                            scores(i, s + AHEAD_S, t)
                        if not (last and s + AHEAD_T >= SLOTS):
                            turn_scores(i, s + AHEAD_T, t)

            turns(pe, TURNS, attend)

            def project_out(b):
                pe.wait_ge(n_low, b + 1)
                by_tokens(0, n_h, n_l, 3).then_inc(proj_done, 1)

            def narrow(b):
                pe.wait_ge(xn3_done, b + 1)
                turn_tokens(xn3, 2).then_inc(xn3_turned, 1)
                pe.wait_ge(xnT_low, b + 1)
                three([(u1_h[:, j, :], u1_l[:, j, :], xnT_h[:, j, :], xnT_l[:, j, :]) for j in range(J)], ps[:, 6, :]).then_inc(rank_done, 1)

            def down(b, f):
                pe.wait_ge(gelu_done, FJ * b + f + 3)
                lo = RANK * (f % 2)
                return nc.tensor.matmul(ps[lo:lo + RANK, 7, :], u2_sb[:, f, :], hT[:, f, :], start=(f < 2), stop=(f >= FJ - 2))

            project_out(0)
            pe.wait_ge(o_read, 2 + 2 * H)
            narrow(0)

            def finish(i, last):
                for u in range(2):
                    b, more = 2 * i + u, not (last and u == 1)
                    if more:
                        pe.wait_ge(x1_done, b + 1)
                        pe.wait_ge(y_done, b + 1)
                        project_out(b + 1)
                    pe.wait_ge(rank_low, b + 1)
                    pe.wait_ge(down_copied, b + 1)
                    for f in range(FJ):
                        pe.wait_ge(gelu_done, FJ * b + f + 1)
                        for n, v1 in enumerate((v1_h, v1_l)):
                            ins = nc.tensor.matmul(ps[:, 4 + f % 2, :], v1[:, f * P:(f + 1) * P], pT[:, :], start=(n == 0), stop=(n == 1))
                        ins.then_inc(ff_done, 1)
                        if f:
                            down(b, f - 1)
                    down(b, FJ - 1).then_inc(down_done, 1)
                    pe.wait_ge(down_copied, b + 2)
                    if more:
                        pe.wait_ge(x1_done, b + 2)
                    else:
                        pe.wait_ge(y_done, b + 1)
                    for t in range(TT):
                        ins = nc.tensor.matmul(ps[:, t // 2, (t % 2) * D:(t % 2 + 1) * D], rT[:, t * P:(t + 1) * P], v2_sb[:, :], start=True, stop=True)
                    ins.then_inc(ffn_done, 1)
                    if more:
                        narrow(b + 1)

            turns(pe, B // 2, finish)


_INS = ['x', 'ctx_1024', 'mask_BxS2_bk1', 'g_xattn', 'g_ffn', 'L0_xattn_relative_bias', 'L0_xattn_Wq', 'L0_xattn_bq',
        'L0_xattn_Wk', 'L0_xattn_bk', 'L0_xattn_Wv', 'L0_xattn_bv', 'L0_xattn_Wo', 'L0_xattn_bo',
        'L0_ffn_U1', 'L0_ffn_V1', 'L0_ffn_b1', 'L0_ffn_U2', 'L0_ffn_V2', 'L0_ffn_b2']


def kernel(**inputs):
    import numpy as _np
    import concourse.bacc as _bacc
    from concourse import mybir as _mybir
    from concourse.bass_utils import run_bass_kernel_spmd as _run

    nc = _bacc.Bacc("TRN2", target_bir_lowering=False, num_devices=1)
    arrays, args = {}, {}
    for name in _INS:
        a = _np.ascontiguousarray(inputs[name])
        arrays[f"in_{name}_dram"] = a
        args[name] = nc.dram_tensor(f"in_{name}_dram", a.shape, _mybir.dt.from_np(a.dtype), kind="ExternalInput").ap()
    out = nc.dram_tensor("out_0_dram", (B, S, D), F32, kind="ExternalOutput").ap()
    qk_parts = nc.dram_tensor("qk_parts_dram", (2, 3, D, B * S), BF16, kind="Internal").ap()
    values = nc.dram_tensor("values_dram", (B, D, S), F32, kind="Internal").ap()
    flamingo_kernel(nc, *[args[n] for n in _INS], out, qk_parts, values)
    r = _run(nc, [arrays], core_ids=[0])
    return r.results[0]["out_0_dram"]
```

```python
from contextlib import ExitStack

import concourse.bass as bass
from concourse import mybir

F32 = mybir.dt.float32
F32R = mybir.dt.float32r
BF16 = mybir.dt.bfloat16
U8 = mybir.dt.uint8
ALU = mybir.AluOpType
ACT = mybir.ActivationFunctionType

P = 128
B, S, D = 8, 512, 256
H, DH = 16, 16
J = D // P
TT = S // P
FF, RANK = 1024, 64
FJ = FF // P
TERMS = 6
ROWS = TERMS * DH
QUERY_PARTS = [(0, 3), (1, 2), (2, 1)]
KEY_PARTS = [(0, 3), (0, 2), (0, 1)]
MASKED = 1.0e30
LOWEST = -3.0e38
EPS = 1.0e-5
SCALE = DH ** -0.5
GROUP = 4
VW = 32
SLOTS = 2 * B
TURNS = H // 2
GROUPS = SLOTS // GROUP
AHEAD_T = GROUP
AHEAD_S = AHEAD_T + 1
EARLY = GROUP
MROW = ROWS

PV_FREE = 1
T_FREE = 4
O_STORES = 16 * GROUP
WARM_UP = 14
WEIGHT_ORDER = (2, 1, 0, 3)
FF_BANKS = 3
STACKS = 16 * (len(QUERY_PARTS) + len(KEY_PARTS))
BATCH_LOADS = 16 * 2
N_CONSTS = 6


def flamingo_kernel(nc, x, ctx_in, mask, g_xattn, g_ffn, rel_bias, Wq, bq, Wk, bk, Wv, bv, Wo, bo,
                    U1, V1, b1, U2, V2, b2, out, qk_parts, values):
    with ExitStack() as ctx:
        def sb(name, shape, dt=F32, stack=ctx):
            return stack.enter_context(nc.sbuf_tensor(name, shape, dt))

        def sem(name):
            return ctx.enter_context(nc.semaphore(name))

        ps = ctx.enter_context(nc.psum_tensor("ps", [P, 8, 512], F32))

        ident = sb("ident", [P, P])
        wT_h = sb("wT_h", [P, 4, J, D], F32R)
        wT_l = sb("wT_l", [P, 4, J, D], F32R)
        u1_h = sb("u1_h", [P, J, 2 * RANK], F32R)
        u1_l = sb("u1_l", [P, J, 2 * RANK], F32R)
        v1_h = sb("v1_h", [P, FF], F32R)
        v1_l = sb("v1_l", [P, FF], F32R)
        u2_sb = sb("u2_sb", [P, FJ, RANK])
        v2_sb = sb("v2_sb", [P, D])
        b1_col = sb("b1_col", [P, FJ])
        qk_b = sb("qk_b", [P, 2, J])
        bv_row = sb("bv_row", [P, D])
        row_b = sb("row_b", [P, 2, D])
        gates = sb("gates", [P, 2])
        eps_pow = sb("eps_pow", [P, 2, TT])
        stats = sb("stats", [P, TT, 6])
        mv = sb("mv", [P, TT, 2])
        rstd = sb("rstd", [P, TT])

        with ExitStack() as phase:
            n_in = sb("n_in", [P, 2, J, S], stack=phase)
            x3 = sb("x3", [P, 2, TT, D], stack=phase)
            x1 = sb("x1", [P, 2, TT, D], stack=phase)
            y_out = sb("y_out", [P, 2, TT, D], stack=phase)
            n_h = sb("n_h", [P, J, S], F32R, stack=phase)
            n_l = sb("n_l", [P, J, S], F32R, stack=phase)
            xn3 = sb("xn3", [P, TT, D], stack=phase)
            xnT_h = sb("xnT_h", [P, J, S], F32R, stack=phase)
            xnT_l = sb("xnT_l", [P, J, S], F32R, stack=phase)
            pT = sb("pT", [P, S], F32R, stack=phase)
            rT = sb("rT", [P, S], stack=phase)
            hT = sb("hT", [P, FJ, S], stack=phase)

        v1_raw = y_out[:, 0].rearrange("p t d -> p (t d)")
        u1_raw = y_out[:, 1, 0, :].rearrange("p (j r) -> p j r", j=J)

        v_all = sb("v_all", [P, H, B * TT, DH])
        bias_sb = sb("bias_sb", [P, 2, TT, S])
        q_st = sb("q_st", [P, 2, B * S], BF16)
        k_st = sb("k_st", [P, 2, B * S], BF16)
        v_win = sb("v_win", [P, 2, B * TT, VW])
        o_sb = sb("o_sb", [P, 2, S])
        o_turned = sb("o_turned", [P, S // VW, VW])
        o_recip = sb("o_recip", [P, S // VW])
        mx = sb("mx", [P, 2, TT])
        mask_u8 = o_sb[:, :, :].rearrange("p u s -> p (u s)").bitcast(U8)

        with ExitStack() as phase:
            x_in = sb("x_in", [P, 2, TT, D], stack=phase)
            c_in = sb("c_in", [P, 2, TT, D], stack=phase)
            xT_h = sb("xT_h", [P, J, S], F32R, stack=phase)
            xT_l = sb("xT_l", [P, J, S], F32R, stack=phase)
            cT_h = sb("cT_h", [P, J, S], F32R, stack=phase)
            cT_l = sb("cT_l", [P, J, S], F32R, stack=phase)
            zf = sb("zf", [P, 2, J, S], stack=phase)
            parts = sb("parts", [P, 2, 2, 3 * J, S], BF16, stack=phase)
            w_raw = sb("w_raw", [P, 4, J, D], stack=phase)
        with ExitStack() as phase:
            p_sb = sb("p_sb", [P, 2 * GROUP, TT, S], stack=phase)
            t_sb = sb("t_sb", [P, 2, TT, S], stack=phase)

        passed_sp = sem("passed_sp")
        passed_dve = sem("passed_dve")
        ident_zero = sem("ident_zero")
        ident_done = sem("ident_done")
        win_zero = sem("win_zero")
        eps_done = sem("eps_done")
        weights_in = [sem(f"weights_in{w}") for w in range(4)]
        biases_in = sem("biases_in")
        consts_in = sem("consts_in")
        mask_in = sem("mask_in")
        bq_scaled = sem("bq_scaled")
        gates_in = sem("gates_in")
        gates_done = sem("gates_done")
        ranks_in = sem("ranks_in")
        rows_done = sem("rows_done")
        wt_done = sem("wt_done")
        wt_high = sem("wt_high")
        wt_low = sem("wt_low")
        ffn_high = sem("ffn_high")
        mask_done = sem("mask_done")
        mask_copied = sem("mask_copied")
        x_loaded = [sem(f"x_loaded{u}") for u in range(2)]
        c_loaded = [sem(f"c_loaded{u}") for u in range(2)]
        half_stats = sem("half_stats")
        moments = sem("moments")
        var_eps = sem("var_eps")
        rstd_done = sem("rstd_done")
        xn_done = sem("xn_done")
        ctx_turned = sem("ctx_turned")
        ctx_high = sem("ctx_high")
        ctx_low = sem("ctx_low")
        x_turned = sem("x_turned")
        x_high = sem("x_high")
        x_low = sem("x_low")
        v_done = sem("v_done")
        v_copied = sem("v_copied")
        qk_done = [sem("q_done"), sem("k_done")]
        qk_copied = [sem("q_copied"), sem("k_copied")]
        rest_done = [sem("q_rest"), sem("k_rest")]
        middle_done = [sem("q_middle"), sem("k_middle")]
        split_done = [sem("q_split"), sem("k_split")]
        parts_stored = [[sem(f"parts_stored{z}{u}") for u in range(2)] for z in range(2)]

        stack_early = [sem(f"stack_early{u}") for u in range(2)]
        stack_in = [sem(f"stack_in{u}") for u in range(2)]
        bias_in = [sem(f"bias_in{u}") for u in range(2)]
        scores_done = sem("scores_done")
        biased = sem("biased")
        lowered_pool = sem("lowered_pool")
        lowered_act = sem("lowered_act")
        turned = sem("turned")
        exp_done = sem("exp_done")
        v_window = sem("v_window")
        pv_done = sem("pv_done")
        o_read = sem("o_read")
        recip_done = sem("recip_done")
        o_scaled = sem("o_scaled")
        o_ready = sem("o_ready")
        o_stored = [sem(f"o_stored{u}") for u in range(2)]

        n_loaded = [sem(f"n_loaded{u}") for u in range(2)]
        n_high = sem("n_high")
        n_low = sem("n_low")
        x_biased = sem("x_biased")
        proj_done = sem("proj_done")
        x1_done = sem("x1_done")
        half_stats3 = sem("half_stats3")
        moments3 = sem("moments3")
        var_eps3 = sem("var_eps3")
        rstd3 = sem("rstd3")
        xn3_done = sem("xn3_done")
        xn3_turned = sem("xn3_turned")
        xnT_high = sem("xnT_high")
        xnT_low = sem("xnT_low")
        rank_done = sem("rank_done")
        rank_high = sem("rank_high")
        rank_low = sem("rank_low")
        ff_done = sem("ff_done")
        gelu_done = sem("gelu_done")
        down_done = sem("down_done")
        down_copied = sem("down_copied")
        ffn_done = sem("ffn_done")
        x1_biased = sem("x1_biased")
        y_done = sem("y_done")
        y_stored = [sem(f"y_stored{u}") for u in range(2)]

        mask_row = mask.rearrange("b s -> (b s)").rearrange("(a s) -> a s", a=1)
        x_v = x.rearrange("b (t p) d -> b p t d", p=P)
        c_v = ctx_in.rearrange("b (t p) d -> b p t d", p=P)
        out_v = out.rearrange("b (t p) d -> b p t d", p=P)
        bias_v = rel_bias.rearrange("o h (t p) k -> (o h) p t k", p=P)
        parts_v = qk_parts.rearrange("z k (j p) s -> z p (k j) s", p=P)
        values_v = values.rearrange("b (j p) s -> b p j s", p=P)

        def turns(eng, n, body):
            with eng.Fori(0, n - 1) as i:
                body(i, False)
            body(n - 1, True)

        def turns_left(eng, n, body):
            with eng.Fori(0, n - 2) as i:
                body(i, 2)
            for left in (1, 0):
                body(n - 1 - left, left)

        def column(v):
            return v.rearrange("(j p) -> p j", p=P)

        def row(v):
            return v.rearrange("(a d) -> a d", a=1).broadcast_to([P, D])

        def number(v):
            return v.rearrange("(a o) -> a o", o=1).broadcast_to([P, 1])

        def head_and_batch(s):
            return s // GROUP % 2, GROUP * (s % SLOTS // (2 * GROUP)) + s % GROUP

        block = ctx.enter_context(nc.Block())

        @block.sync
        def _(sp):
            def load_weight(w, src):
                sp.dma_start(w_raw[:, w], src.rearrange("(j p) d -> p j d", p=P)).then_inc(weights_in[w], 16)

            def load_bias(h, u):
                sp.dma_start(bias_sb[:, u], bias_v[bass.ds(h, 1)].rearrange("o p t k -> (o p) t k")).then_inc(bias_in[u], 16)

            def load_stacks(h, u, lo, hi, loaded):
                rows, cols = bass.ds(h * DH, DH), slice(lo * S, hi * S)
                row = 0
                for part, times in QUERY_PARTS:
                    src = qk_parts[0, part:part + 1, rows, cols].broadcast_to([times, DH, (hi - lo) * S])
                    sp.dma_start(q_st[row:row + times * DH, u, cols], src).then_inc(loaded, 16)
                    row += times * DH
                row = 0
                for part, n in KEY_PARTS:
                    sp.dma_start(k_st[row:row + n * DH, u, cols], qk_parts[1, part:part + n, rows, cols]).then_inc(loaded, 16)
                    row += n * DH

            load_weight(2, Wv)
            sp.dma_start(c_in[:, 0], c_v[0]).then_inc(c_loaded[0], 16)
            load_weight(1, Wk)
            load_weight(0, Wq)
            sp.dma_start(mask_u8[MROW:MROW + 1, :], mask_row).then_inc(mask_in, 16)
            with nc.allow_non_contiguous_dma(reason="columns of a few numbers"):
                for dst, src in ((bv_row[:, :], row(bv)), (qk_b[:, 0, :], column(bq)), (qk_b[:, 1, :], column(bk))):
                    sp.dma_start(dst, src).then_inc(biases_in, 16)
                load_weight(3, Wo)
                sp.dma_start(c_in[:, 1], c_v[1]).then_inc(c_loaded[1], 16)
                sp.wait_ge(x_turned, 1)
                loads = [(row_b[:, 0, :], row(bo)), (row_b[:, 1, :], row(b2)),
                         (u2_sb[:, :, :], U2.rearrange("(f p) r -> p f r", p=P)),
                         (v2_sb[0:RANK, :], V2), (v2_sb[RANK:P, :], V2),
                         (b1_col[:, :], b1.rearrange("(f p) -> p f", p=P))]
                assert len(loads) == N_CONSTS
                for dst, src in loads:
                    sp.dma_start(dst, src).then_inc(consts_in, 16)
            load_bias(0, 0)
            sp.wait_ge(mask_done, 2)
            for rows in (q_st, k_st):
                sp.dma_start(rows[MROW:MROW + 1, 1, :], rows[MROW:MROW + 1, 0, :]).then_inc(mask_copied, 16)

            def project(i, last):
                if last:
                    for z in range(2):
                        for u in range(2):
                            sp.wait_ge(parts_stored[z][u], 16 + 16 * (EARLY // 2))
                    for u in range(2):
                        load_stacks(u, u, 0, EARLY, stack_early[u])
                    load_bias(1, 1)
                for u in range(2):
                    b = 2 * i + u
                    for z in (1, 0):
                        sp.wait_ge(split_done[z], b + 2)
                        sp.sem_inc(passed_sp, 1)
                        sp.dma_start(parts_v[z][:, :, bass.ds(b * S, S)], parts[:, z, u]).then_inc(parts_stored[z][u], 16)

            turns(sp, B // 2, project)
            for z in range(2):
                for u in range(2):
                    sp.wait_ge(parts_stored[z][u], 16 + 16 * (B // 2))
            for u in range(2):
                load_stacks(u, u, EARLY, B, stack_in[u])

            def store_values(i, k):
                u, half, w = k % 2, k // 2, k % 2
                sp.wait_ge(o_ready, GROUPS * i + k + 1)
                sp.sem_inc(passed_sp, 1)
                for g in range(GROUP):
                    sp.dma_start(values[GROUP * half + g, bass.ds((2 * i + u) * DH, DH), :],
                                 o_sb[VW * g:VW * g + DH, w, :]).then_inc(o_stored[w], 16)

            def attend(i, last):
                for k in range(GROUPS):
                    store_values(i, k)
                    if k < 2 and not last:
                        sp.wait_ge(biased, TT * (SLOTS * i + GROUP * (k + 3)))
                        sp.sem_inc(passed_sp, 1)
                        load_bias(2 * i + k + 2, k)
                        load_stacks(2 * i + k + 2, k, 0, B, stack_in[k])
                    if k == 0 and last:
                        sp.wait_ge(v_window, H)
                        for dst, src in ((v1_raw[0:RANK, :], V1), (v1_raw[RANK:P, :], V1)):
                            sp.dma_start(dst, src).then_inc(ranks_in, 16)
                        for n in range(2):
                            sp.dma_start(u1_raw[:, :, n * RANK:(n + 1) * RANK], U1.rearrange("(j p) r -> p j r", p=P)).then_inc(ranks_in, 16)
                    if k == 1 and last:
                        for w in range(2):
                            sp.wait_ge(o_stored[w], O_STORES * H)
                        load_batch(0, 0)
                        load_batch(1, 1)

            def load_batch(b, u):
                sp.dma_start(n_in[:, u], values_v[bass.ds(b, 1)].rearrange("o p j s -> (o p) j s")).then_inc(n_loaded[u], 16)
                sp.dma_start(x3[:, u], x_v[bass.ds(b, 1)].rearrange("o p t d -> (o p) t d")).then_inc(n_loaded[u], 16)

            turns(sp, TURNS, attend)

            def finish(i, last):
                for u in range(2):
                    b = 2 * i + u
                    if not last:
                        if u == 1:
                            for w in range(2):
                                sp.wait_ge(o_stored[w], O_STORES * (H + 1))
                        sp.wait_ge(n_low, b + 1)
                        sp.wait_ge(x1_done, b + 1)
                        sp.sem_inc(passed_sp, 1)
                        load_batch(b + 2, u)
                    for k in range(2):
                        sp.wait_ge(y_done, 2 * b + k + 1)
                        sp.sem_inc(passed_sp, 1)
                        sp.dma_start(out_v[bass.ds(b, 1), :, 2 * k:2 * k + 2].rearrange("o p t d -> (o p) t d"),
                                     y_out[:, u, 2 * k:2 * k + 2]).then_inc(y_stored[u], 16)

            turns(sp, B // 2, finish)
            for u in range(2):
                sp.wait_ge(y_stored[u], 32 * (B // 2 + 1))

        @block.gpsimd
        def _(pool):
            nc.gpsimd.memset(ident[:, :], 0.0).then_inc(ident_zero, 1)
            pool.wait_ge(ident_zero, 1)
            nc.gpsimd.affine_select(out=ident[:, :], in_=ident[:, :], compare_op=ALU.not_equal, fill=1.0, base=0,
                                    pattern=[[-1, P]], channel_multiplier=1).then_inc(ident_done, 1)
            for s in (*qk_copied, *split_done):
                pool.sem_inc(s, 1)
            for s, n in ((o_read, 2), (turned, T_FREE), (pv_done, PV_FREE)):
                pool.sem_inc(s, n)
            for u in range(2):
                for z in range(2):
                    pool.sem_inc(parts_stored[z][u], 16)
                pool.sem_inc(o_stored[u], O_STORES)
                pool.sem_inc(y_stored[u], 32)
            nc.gpsimd.memset(eps_pow[:, 0, :], EPS)
            nc.gpsimd.memset(eps_pow[:, 1, :], -0.5).then_inc(eps_done, 1)
            pool.wait_ge(eps_done, 1)

            def reciprocal_root(b, ready, out_ap, var, done_eps, done):
                pool.wait_ge(ready, b + 1)
                nc.gpsimd.tensor_tensor(out_ap, var, eps_pow[:, 0, :], ALU.add).then_inc(done_eps, 1)
                pool.wait_ge(done_eps, b + 1)
                nc.gpsimd.tensor_tensor(out_ap, out_ap, eps_pow[:, 1, :], ALU.pow).then_inc(done, 1)

            def low_part(z, b, u):
                pool.wait_ge(middle_done[z], b + 1)
                nc.gpsimd.tensor_tensor(parts[:, z, u, 2 * J:3 * J, :], zf[:, z], parts[:, z, u, J:2 * J, :],
                                        ALU.subtract).then_inc(split_done[z], 1)

            reciprocal_root(0, moments, rstd[:, :], mv[:, :, 1], var_eps, rstd_done)
            pool.wait_ge(mask_in, 16)
            pool.wait_ge(rstd_done, 1)
            nc.gpsimd.tensor_scalar(k_st[MROW:MROW + 1, 0, :], mask_u8[MROW:MROW + 1, :], MASKED, -MASKED, ALU.mult, ALU.add).then_inc(mask_done, 1)
            pool.wait_ge(mask_done, 1)
            reciprocal_root(1, moments, rstd[:, :], mv[:, :, 1], var_eps, rstd_done)
            pool.wait_ge(rstd_done, 2)
            nc.gpsimd.memset(q_st[MROW:MROW + 1, 0, :], 1.0).then_inc(mask_done, 1)
            pool.wait_ge(mask_done, 2)
            for u in range(2):
                nc.gpsimd.memset(v_win[:, u], 0.0).then_inc(win_zero, 1)
            pool.wait_ge(win_zero, 2)
            nc.gpsimd.memset(v_win[:, :, :, DH:DH + 1], 1.0).then_inc(win_zero, 1)
            pool.wait_ge(win_zero, 3)

            def project(i, last):
                for u in range(2):
                    b = 2 * i + u
                    if not last:
                        reciprocal_root(b + 2, moments, rstd[:, :], mv[:, :, 1], var_eps, rstd_done)
                    if not (last and u == 1):
                        low_part(1, b, u)
                        low_part(0, b, u)

            def take_values(h, u):
                nc.gpsimd.tensor_copy(v_win[:, u, :, 0:DH], v_all[:, bass.ds(h, 1), :, :].rearrange("p o t d -> p (o t) d")).then_inc(v_window, 1)

            def lower(i, s, t):
                pool.wait_ge(biased, TT * (SLOTS * i + s) + t + 1)
                ins = nc.gpsimd.tensor_tensor(t_sb[:, s % 2, t, :], mx[:, s % 2, t:t + 1].broadcast_to([P, S]),
                                              t_sb[:, s % 2, t, :], ALU.subtract)
                if t == 1:
                    ins.then_inc(lowered_pool, 1)

            def divide(k):
                pool.wait_ge(recip_done, k + 1)
                nc.gpsimd.tensor_tensor(o_turned[:, :, 0:DH], o_turned[:, :, 0:DH],
                                        o_recip[:, :].rearrange("p (k o) -> p k o", o=1).broadcast_to([P, S // VW, DH]),
                                        ALU.mult).then_inc(o_scaled, 1)

            turns(pool, B // 2, project)
            for s in range(AHEAD_S):
                for t in range(2):
                    lower(0, s, t)
                if s == 2:
                    pool.wait_ge(v_copied, B)
                    take_values(0, 0)

            def bias_tokens(b, i, u):
                pool.wait_ge(n_loaded[u], BATCH_LOADS * (i + 1))
                row = row_b[:, 0:1, :].broadcast_to([P, TT, D])
                nc.gpsimd.tensor_tensor(x3[:, u], x3[:, u], row, ALU.add).then_inc(x_biased, 1)

            def attend(i, last):
                for s in range(SLOTS - GROUP if last else SLOTS):
                    for t in range(2):
                        if not (last and s + AHEAD_S >= SLOTS):
                            lower(i, s + AHEAD_S, t)
                        if t == 1 and s % GROUP == GROUP - 1:
                            divide(GROUPS * i + s // GROUP)
                    if s == 0:
                        pool.wait_ge(pv_done, GROUPS * i + PV_FREE)
                        take_values(2 * i + 1, 1)
                    if s == 3 * GROUP:
                        pool.wait_ge(pv_done, GROUPS * i + 3 + PV_FREE)
                        take_values(2 * i + 2, 0)
                    if last and s + AHEAD_S == SLOTS - 1:
                        pool.wait_ge(rows_done, 1)
                        bias_tokens(0, 0, 0)

            turns(pool, TURNS, attend)

            def bias_result(b, u):
                pool.wait_ge(xn3_done, b + 1)
                row = row_b[:, 1:2, :].broadcast_to([P, TT, D])
                nc.gpsimd.tensor_tensor(x1[:, u], x1[:, u], row, ALU.add).then_inc(x1_biased, 1)

            pool.wait_ge(n_high, 2)
            nc.gpsimd.tensor_tensor(n_l[:, :, :], n_in[:, 1], n_h[:, :, :].bitcast(F32), ALU.subtract).then_inc(n_low, 1)
            reciprocal_root(0, moments3, rstd[:, :], mv[:, :, 1], var_eps3, rstd3)
            bias_tokens(1, 0, 1)
            divide(2 * H - 1)
            bias_result(0, 0)

            def finish(i, last):
                for u in range(2):
                    b, v = 2 * i + u, 1 - u
                    if not (last and u == 1):
                        reciprocal_root(b + 1, moments3, rstd[:, :], mv[:, :, 1], var_eps3, rstd3)
                    if not last:
                        bias_tokens(b + 2, i + 1, u)
                    if not (last and u == 1):
                        bias_result(b + 1, v)

            turns(pool, B // 2, finish)

        @block.scalar
        def _(act):
            def copy(dst, src):
                return nc.scalar.activation(dst, src, ACT.Identity)

            for n, gate in enumerate((g_xattn, g_ffn)):
                act.dma_start(gates[:, n:n + 1], number(gate)).then_inc(gates_in, 16)
            act.dma_start(x_in[:, 0], x_v[0]).then_inc(x_loaded[0], 16)
            act.dma_start(x_in[:, 1], x_v[1]).then_inc(x_loaded[1], 16)
            act.wait_ge(gates_in, 32)
            nc.scalar.activation(gates[:, :], gates[:, :], ACT.Tanh).then_inc(gates_done, 1)

            def turn_high(w):
                act.wait_ge(wt_done, w + 1)
                n = WEIGHT_ORDER[w]
                copy(wT_h[:, n].rearrange("p j d -> p (j d)"), ps[:, 4 + w, :]).then_inc(wt_high, 1)

            def ctx_parts(b):
                act.wait_ge(ctx_turned, b + 1)
                copy(cT_h[:, :, :], ps[:, 0:2, :]).then_inc(ctx_high, 1)

            def x_parts(b):
                act.wait_ge(x_turned, b + 1)
                copy(xT_h[:, :, :], ps[:, 2:4, :]).then_inc(x_high, 1)

            def load_ctx(b, u):
                act.dma_start(c_in[:, u], c_v[bass.ds(b, 1)].rearrange("o p t d -> (o p) t d")).then_inc(c_loaded[u], 16)

            def load_x(b, u):
                act.dma_start(x_in[:, u], x_v[bass.ds(b, 1)].rearrange("o p t d -> (o p) t d")).then_inc(x_loaded[u], 16)

            turn_high(0)
            ctx_parts(0)
            load_ctx(2, 0)
            turn_high(1)
            turn_high(2)
            turn_high(3)
            x_parts(0)
            load_x(2, 0)
            act.wait_ge(bq_scaled, 1)

            def high_part(z, b, i, u):
                bank, scale = ((6, SCALE), (4, 1.0))[z]
                act.wait_ge(qk_done[z], b + 1)
                act.wait_ge(parts_stored[z][u], 16 * (i + 1))
                for j in range(J):
                    nc.scalar.activation(parts[:, z, u, j, :], ps[:, bank + j, :], ACT.Identity, bias=qk_b[:, z, j:j + 1], scale=scale)
                act.wait_ge(split_done[z], b + 1)
                for j in range(J):
                    ins = nc.scalar.activation(zf[:, z, j, :], ps[:, bank + j, :], ACT.Identity, bias=qk_b[:, z, j:j + 1], scale=scale)
                ins.then_inc(qk_copied[z], 1)

            def middle_part(z, b, u):
                act.wait_ge(rest_done[z], b + 1)
                copy(parts[:, z, u, J:2 * J, :], zf[:, z]).then_inc(middle_done[z], 1)

            def lower(i, s, t):
                act.wait_ge(biased, TT * (SLOTS * i + s) + t + 1)
                ins = nc.scalar.activation(t_sb[:, s % 2, t, :], t_sb[:, s % 2, t, :], ACT.Identity, bias=mx[:, s % 2, t:t + 1], scale=-1.0)
                if t == TT - 1:
                    ins.then_inc(lowered_act, 1)

            def project(i, left):
                for u in range(2):
                    b, more = 2 * i + u, u < 2 * left + 1
                    if more:
                        ctx_parts(b + 1)
                    if u + 1 < 2 * left:
                        load_ctx(b + 3, 1 - u)
                    high_part(1, b, i, u)
                    if more:
                        x_parts(b + 1)
                    if u + 1 < 2 * left:
                        load_x(b + 3, 1 - u)
                    if not more:
                        for t in range(2, TT):
                            lower(0, 0, t)
                    high_part(0, b, i, u)
                    if more:
                        middle_part(1, b, u)
                        middle_part(0, b, u)

            turns_left(act, B // 2, project)

            def exponentials(i, s, p, free=True):
                act.wait_ge(turned, 2 * (SLOTS * i + s) + p + 1 + T_FREE)
                if free and p == 0:
                    act.wait_ge(pv_done, GROUPS * i + s // GROUP - 1 + PV_FREE)
                nc.scalar.activation(p_sb[:, s % (2 * GROUP), 2 * p:2 * p + 2, :], ps[:, 2 + 2 * p:4 + 2 * p, :], ACT.Exp, scale=-1.0).then_inc(exp_done, 1)

            act.wait_ge(qk_done[0], B)
            for s in range(AHEAD_T):
                if s < 2:
                    middle_part(1 - s, B - 1, 1)
                for p in range(2):
                    lower(0, s + 1, 2 + p)
                    exponentials(0, s, p, free=False)
            for z in range(2):
                act.wait_ge(split_done[z], B + 1)
                for u in range(2):
                    act.wait_ge(parts_stored[z][u], 16 * (B // 2 + 1))

            def split_values(b, i, u):
                act.wait_ge(n_loaded[u], BATCH_LOADS * (i + 1))
                act.wait_ge(proj_done, b)
                copy(n_h[:, :, :], n_in[:, u]).then_inc(n_high, 1)

            def attend(i, last):
                for s in range(SLOTS - GROUP if last else SLOTS):
                    soon = s % GROUP == GROUP - 1
                    if soon:
                        exponentials(i, s + AHEAD_T, 0)
                    for p in range(2):
                        if not (last and s + AHEAD_S >= SLOTS):
                            lower(i, s + AHEAD_S, 2 + p)
                        if p or not soon:
                            exponentials(i, s + AHEAD_T, p)

            turns(act, TURNS, attend)

            def narrow(b):
                for j in range(J):
                    act.wait_ge(xn3_turned, J * b + j + 1)
                    copy(xnT_h[:, j, :], ps[:, 2 + j, :]).then_inc(xnT_high, 1)
                act.wait_ge(rank_done, b + 1)
                copy(pT[:, :], ps[:, 6, :]).then_inc(rank_high, 1)

            act.wait_ge(ranks_in, 64)
            act.wait_ge(consts_in, 16 * N_CONSTS)
            copy(u1_h[:, :, :], u1_raw)
            copy(v1_h[:, :], v1_raw).then_inc(ffn_high, 1)
            split_values(1, 0, 1)
            narrow(0)

            def finish(i, last):
                for u in range(2):
                    b = 2 * i + u
                    for f in range(FJ):
                        act.wait_ge(ff_done, FJ * b + f + 1)
                        nc.scalar.activation(hT[:, f, :], ps[:, 4 + f % FF_BANKS, :], ACT.Gelu_apprx_tanh, bias=b1_col[:, f:f + 1]).then_inc(gelu_done, 1)
                        if f == FJ // 2 and not last:
                            split_values(b + 2, i + 1, u)
                    act.wait_ge(down_done, b + 1)
                    copy(rT[:, :], ps[:, 7, :]).then_inc(down_copied, 1)
                    if not (last and u == 1):
                        narrow(b + 1)

            turns(act, B // 2, finish)

        @block.vector
        def _(dve):
            def less(dst, src, high):
                return nc.vector.tensor_tensor(dst, src, high.bitcast(F32), ALU.subtract)

            def statistics(b, src, ready, want, stats_done, done):
                dve.wait_ge(ready, want)
                for t in range(TT):
                    ins = nc.vector.bn_stats(stats[:, t, :], src[:, t, :])
                ins.then_inc(stats_done, 1)
                dve.wait_ge(stats_done, b + 1)
                dve.sem_inc(passed_dve, 1)
                for t in range(TT):
                    ins = nc.vector.bn_aggr(mv[:, t, :], stats[:, t, :])
                ins.then_inc(done, 1)

            def normalise(b, dst, src, root_done, done):
                dve.wait_ge(root_done, b + 1)
                for t in range(TT):
                    ins = nc.vector.tensor_scalar(dst[:, t, :], src[:, t, :], mv[:, t, 0:1], rstd[:, t:t + 1], ALU.subtract, ALU.mult)
                ins.then_inc(done, 1)

            def turn_low(w):
                dve.wait_ge(wt_high, w + 1)
                n = WEIGHT_ORDER[w]
                less(wT_l[:, n].rearrange("p j d -> p (j d)"), ps[:, 4 + w, :], wT_h[:, n].rearrange("p j d -> p (j d)")).then_inc(wt_low, 1)

            def ctx_parts(b):
                dve.wait_ge(ctx_high, b + 1)
                less(cT_l[:, :, :], ps[:, 0:2, :], cT_h[:, :, :]).then_inc(ctx_low, 1)

            def x_parts(b):
                dve.wait_ge(x_high, b + 1)
                less(xT_l[:, :, :], ps[:, 2:4, :], xT_h[:, :, :]).then_inc(x_low, 1)

            def rest(z, b, u):
                dve.wait_ge(qk_copied[z], b + 2)
                nc.vector.tensor_tensor(zf[:, z], zf[:, z], parts[:, z, u, 0:J, :], ALU.subtract).then_inc(rest_done[z], 1)

            def copy_values(b):
                dve.wait_ge(v_done, b + 1)
                for k in range(2):
                    ins = nc.vector.tensor_tensor(v_all[:, :, bass.ds(TT * b + 2 * k, 2), :].rearrange("p h t d -> p t h d"),
                                                  ps[:, k, :].rearrange("p (t h d) -> p t h d", t=2, h=H),
                                                  bv_row[:, :].rearrange("p (o h d) -> p o h d", o=1, h=H).broadcast_to([P, 2, H, DH]),
                                                  ALU.add)
                ins.then_inc(v_copied, 1)

            def ffn_weights():
                dve.wait_ge(ffn_high, 1)
                less(u1_l[:, :, :], u1_raw, u1_h[:, :, :])
                less(v1_l[:, :], v1_raw, v1_h[:, :])

            def gate_rows():
                dve.wait_ge(gates_done, 1)
                dve.wait_ge(consts_in, 16 * N_CONSTS)
                for n in range(2):
                    ins = nc.vector.tensor_scalar(row_b[:, n, :], row_b[:, n, :], gates[:, n:n + 1], None, ALU.mult)
                ins.then_inc(rows_done, 1)

            turn_low(0)
            ctx_parts(0)
            statistics(0, x_in[:, 0], x_loaded[0], 16, half_stats, moments)
            turn_low(1)
            normalise(0, x_in[:, 0], x_in[:, 0], rstd_done, xn_done)
            dve.wait_ge(biases_in, 48)
            nc.vector.tensor_scalar(qk_b[:, 0, :], qk_b[:, 0, :], SCALE, None, ALU.mult).then_inc(bq_scaled, 1)
            copy_values(0)
            turn_low(2)
            turn_low(3)
            statistics(1, x_in[:, 1], x_loaded[1], 16, half_stats, moments)
            x_parts(0)
            normalise(1, x_in[:, 1], x_in[:, 1], rstd_done, xn_done)

            def bias_scores(i, s, t):
                u, n = s // GROUP % 2, TT * (SLOTS * i + s) + t
                if t == 0:
                    if s % SLOTS in (0, GROUP):
                        dve.wait_ge(bias_in[u], 16 * (i + s // SLOTS + 1))
                    dve.wait_ge(turned, 2 * (SLOTS * i + s) + 2)
                dve.wait_ge(scores_done, n + 1)
                dve.sem_inc(passed_dve, 1)
                nc.vector.tensor_tensor_reduce(out=t_sb[:, s % 2, t, :], in0=ps[:, t % 2, :], in1=bias_sb[:, u, t, :], scale=1.0,
                                               scalar=LOWEST, op0=ALU.add, op1=ALU.max, accum_out=mx[:, s % 2, t:t + 1]).then_inc(biased, 1)

            def project(i, last):
                for u in range(2):
                    b, more = 2 * i + u, not (last and u == 1)
                    if more:
                        ctx_parts(b + 1)
                    if not last:
                        statistics(b + 2, x_in[:, u], x_loaded[u], 16 * (i + 2), half_stats, moments)
                    if more:
                        rest(1, b, u)
                        x_parts(b + 1)
                        copy_values(b + 1)
                    else:
                        for t in range(TT):
                            bias_scores(0, 0, t)
                        rest(1, b, u)
                        for t in range(TT):
                            bias_scores(0, 1, t)
                    rest(0, b, u)
                    if not more:
                        for s, z in ((2, 1), (3, 0)):
                            for t in range(TT):
                                bias_scores(0, s, t)
                            dve.wait_ge(middle_done[z], B)
                            nc.vector.tensor_tensor(parts[:, z, u, 2 * J:3 * J, :], zf[:, z], parts[:, z, u, J:2 * J, :],
                                                    ALU.subtract).then_inc(split_done[z], 1)
                    if not last:
                        normalise(b + 2, x_in[:, u], x_in[:, u], rstd_done, xn_done)

            turns(dve, B // 2, project)

            for s in range(4, AHEAD_S + 1):
                for t in range(TT):
                    bias_scores(0, s, t)

            def read_values(i, k):
                dve.wait_ge(pv_done, GROUPS * i + k + 1 + PV_FREE)
                nc.vector.transpose(o_turned[:, :, :].rearrange("p k c -> p (k c)"), ps[:, 6 + k % 2, :]).then_inc(o_read, 1)

            def invert_sums(i, k):
                dve.wait_ge(o_read, GROUPS * i + k + 3)
                nc.vector.reciprocal(o_recip[:, :], o_turned[:, :, DH]).then_inc(recip_done, 1)

            def turn_values(i, k):
                dve.wait_ge(o_scaled, GROUPS * i + k + 1)
                dve.wait_ge(o_stored[k % 2], O_STORES * (2 * i + k // 2 + 1))
                nc.vector.transpose(o_sb[:, k % 2, :], o_turned[:, :, :].rearrange("p k c -> p (k c)")).then_inc(o_ready, 1)

            def split_values(b, u):
                dve.wait_ge(n_high, b + 1)
                less(n_l[:, :, :], n_in[:, u], n_h[:, :, :]).then_inc(n_low, 1)

            def attend(i, last):
                for s in range(1, SLOTS - GROUP + 1 if last else SLOTS + 1):
                    if last and s == 2 * GROUP + 1:
                        gate_rows()
                    for t in range(TT):
                        if not (last and s + AHEAD_S >= SLOTS):
                            bias_scores(i, s + AHEAD_S, t)
                        if s % GROUP == GROUP - 1 and t == 1:
                            read_values(i, s // GROUP)
                        if s % GROUP == GROUP - 1 and t == 3:
                            invert_sums(i, s // GROUP)
                        if s % GROUP == 0 and t == 1:
                            turn_values(i, s // GROUP - 1)
                    if last and s + AHEAD_S == SLOTS - 1:
                        dve.wait_ge(n_loaded[0], BATCH_LOADS)
                        nc.vector.tensor_copy(n_h[:, :, :], n_in[:, 0]).then_inc(n_high, 1)
                        split_values(0, 0)

            turns(dve, TURNS, attend)

            def residual(b, u):
                dve.wait_ge(proj_done, b + 1)
                dve.wait_ge(x_biased, b + 1)
                nc.vector.scalar_tensor_tensor(out=x1[:, u].rearrange("p t d -> p (t d)"), in0=ps[:, 0:2, :].rearrange("p k s -> p (k s)"),
                                               scalar=gates[:, 0:1], in1=x3[:, u].rearrange("p t d -> p (t d)"),
                                               op0=ALU.mult, op1=ALU.add).then_inc(x1_done, 1)

            def narrow(b):
                for j in range(J):
                    dve.wait_ge(xnT_high, J * b + j + 1)
                    less(xnT_l[:, j, :], ps[:, 2 + j, :], xnT_h[:, j, :]).then_inc(xnT_low, 1)

            def narrow_rank(b):
                dve.wait_ge(rank_high, b + 1)
                less(pT[RANK:P, :], ps[RANK:P, 6, :], pT[RANK:P, :]).then_inc(rank_low, 1)

            residual(0, 0)
            statistics(0, x1[:, 0], x1_done, 1, half_stats3, moments3)
            ffn_weights()
            normalise(0, xn3, x1[:, 0], rstd3, xn3_done)
            read_values(TURNS - 1, GROUPS - 1)
            invert_sums(TURNS - 1, GROUPS - 1)
            narrow(0)
            turn_values(TURNS - 1, GROUPS - 1)
            narrow_rank(0)

            def finish(i, last):
                for u in range(2):
                    b, v, more = 2 * i + u, 1 - u, not (last and u == 1)
                    if more:
                        residual(b + 1, v)
                        statistics(b + 1, x1[:, v], x1_done, b + 2, half_stats3, moments3)
                        dve.wait_ge(xn3_turned, J * (b + 1))
                        normalise(b + 1, xn3, x1[:, v], rstd3, xn3_done)
                    if not last:
                        split_values(b + 2, u)
                    if more:
                        narrow(b + 1)
                    dve.wait_ge(x1_biased, b + 1)
                    dve.wait_ge(y_stored[u], 32 * (i + 1))
                    for k in range(2):
                        dve.wait_ge(ffn_done, 2 * b + k + 1)
                        nc.vector.scalar_tensor_tensor(out=y_out[:, u, 2 * k:2 * k + 2], in0=ps[:, k, :].rearrange("p (t d) -> p t d", t=2),
                                                       scalar=gates[:, 1:2], in1=x1[:, u, 2 * k:2 * k + 2],
                                                       op0=ALU.mult, op1=ALU.add).then_inc(y_done, 1)
                    if more:
                        narrow_rank(b + 1)

            turns(dve, B // 2, finish)

        @block.tensor
        def _(pe):
            def turn_weight(w):
                n = WEIGHT_ORDER[w]
                pe.wait_ge(weights_in[n], 16)
                for jo in range(J):
                    for ji in range(J):
                        lo = ji * D + jo * P
                        ins = nc.tensor.transpose(ps[:, 4 + w, lo:lo + P], w_raw[:, n, jo, ji * P:(ji + 1) * P], ident[:, :])
                ins.then_inc(wt_done, 1)

            def turn_tokens(src, bank):
                for j in range(J):
                    for t in range(TT):
                        ins = nc.tensor.transpose(ps[:, bank + j, t * P:(t + 1) * P], src[:, t, j * P:(j + 1) * P], ident[:, :])
                return ins

            def three(pairs, dst):
                terms = [(a, b) for a_h, a_l, b_h, b_l in pairs for a, b in ((a_h, b_h), (a_h, b_l), (a_l, b_h))]
                for n, (a, b) in enumerate(terms):
                    ins = nc.tensor.matmul(dst, a, b, start=(n == 0), stop=(n == len(terms) - 1))
                return ins

            def by_tokens(bank, src_h, src_l, w, tiles=range(TT)):
                for t in tiles:
                    cols = slice(t * P, (t + 1) * P)
                    ins = three([(src_h[:, j, cols], src_l[:, j, cols], wT_h[:, w, j, :], wT_l[:, w, j, :]) for j in range(J)],
                                ps[:, bank + t // 2, (t % 2) * D:(t % 2 + 1) * D])
                return ins

            def by_width(bank, w, src_h, src_l, halves=range(J)):
                for jo in halves:
                    cols = slice(jo * P, (jo + 1) * P)
                    ins = three([(wT_h[:, w, j, cols], wT_l[:, w, j, cols], src_h[:, j, :], src_l[:, j, :]) for j in range(J)],
                                ps[:, bank + jo, :])
                return ins

            pe.wait_ge(ident_done, 1)
            for n in range(WARM_UP):
                nc.tensor.transpose(ps[:, 7, 0:P], ident[:, :], ident[:, :])
            turn_weight(0)
            pe.wait_ge(c_loaded[0], 16)
            turn_tokens(c_in[:, 0], 0).then_inc(ctx_turned, 1)
            turn_weight(1)

            def project_values(b):
                pe.wait_ge(ctx_low, b + 1)
                by_tokens(0, cT_h, cT_l, 2).then_inc(v_done, 1)

            pe.wait_ge(wt_low, 1)
            project_values(0)
            turn_weight(2)
            turn_weight(3)
            pe.wait_ge(xn_done, 1)
            turn_tokens(x_in[:, 0], 2).then_inc(x_turned, 1)

            def scores(i, s, t):
                (u, b), n = head_and_batch(s), TT * (SLOTS * i + s) + t
                if s % GROUP == 0 and t == 0 and s >= AHEAD_S:
                    pe.wait_ge(stack_in[u], STACKS * (i + s // SLOTS + 1))
                if s or t >= 2:
                    pe.wait_ge(biased, n - 1)
                lo = b * S + t * P
                nc.tensor.matmul(ps[:, t % 2, :], q_st[0:MROW + 1, u, lo:lo + P], k_st[0:MROW + 1, u, b * S:(b + 1) * S],
                                 start=True, stop=True).then_inc(scores_done, 1)

            def project(i, last):
                for u in range(2):
                    b, v, more = 2 * i + u, 1 - u, not (last and u == 1)
                    pe.wait_ge(wt_low, 2)
                    pe.wait_ge(qk_copied[1], b + 1)
                    by_width(4, 1, cT_h, cT_l).then_inc(qk_done[1], 1)
                    if more:
                        pe.wait_ge(c_loaded[v], 16 * (i + u + 1))
                        pe.wait_ge(v_copied, b + 1)
                        turn_tokens(c_in[:, v], 0).then_inc(ctx_turned, 1)
                    pe.wait_ge(x_low, b + 1)
                    pe.wait_ge(wt_low, 4)
                    pe.wait_ge(qk_copied[0], b + 1)
                    if more:
                        by_width(6, 0, xT_h, xT_l).then_inc(qk_done[0], 1)
                    else:
                        pe.wait_ge(mask_copied, 32)
                        pe.wait_ge(v_copied, B)
                        pe.wait_ge(stack_early[0], STACKS)
                        for t in range(2):
                            scores(0, 0, t)
                        by_width(6, 0, xT_h, xT_l, halves=(0,))
                        for t in range(2, TT):
                            scores(0, 0, t)
                        by_width(6, 0, xT_h, xT_l, halves=(1,)).then_inc(qk_done[0], 1)
                    if more:
                        pe.wait_ge(xn_done, b + 2)
                        turn_tokens(x_in[:, v], 2).then_inc(x_turned, 1)
                        project_values(b + 1)

            turns(pe, B // 2, project)

            def turn_scores(i, s, k, free=True):
                w, g = s % 2, SLOTS * i + s
                if k == 0:
                    pe.wait_ge(lowered_pool, g + 1)
                    pe.wait_ge(lowered_act, g + 1)
                if k % 2 == 0 and free:
                    pe.wait_ge(exp_done, 2 * g + k // 2 - 1)
                for t in range(TT):
                    ins = nc.tensor.transpose(ps[:, 2 + k, t * P:(t + 1) * P], t_sb[:, w, t, k * P:(k + 1) * P], ident[:, :])
                if k % 2:
                    ins.then_inc(turned, 1)

            def weigh(i, s):
                (h, first), k, t, bank = head_and_batch(s - s % GROUP), GROUPS * i + s // GROUP, s % GROUP, 6 + s // GROUP % 2
                if t == 0:
                    pe.wait_ge(v_window, 2 * i + h + 1)
                    pe.wait_ge(o_read, k + 1)
                if t % 2 == 0:
                    pe.wait_ge(exp_done, 2 * GROUP * (k + 1) - 1 + t // 2)
                for g in range(GROUP):
                    ins = nc.tensor.matmul(ps[VW * g:VW * (g + 1), bank, :], v_win[:, h, (first + g) * TT + t, :],
                                           p_sb[:, (s - t + g) % (2 * GROUP), t, :],
                                           start=(t == 0), stop=(t == TT - 1))
                if t == TT - 1:
                    ins.then_inc(pv_done, 1)

            pe.wait_ge(qk_copied[1], B + 1)
            for s in range(AHEAD_T):
                if s + 1 == GROUP:
                    pe.wait_ge(stack_early[1], STACKS)
                for t in range(2):
                    scores(0, s + 1, t)
                if s:
                    scores(0, s + 1, 2)
                turn_scores(0, s, 0, free=s > 0)
                if not s:
                    scores(0, s + 1, 2)
                scores(0, s + 1, 3)
                for k in range(1, TT):
                    turn_scores(0, s, k, free=s > 0)
            pe.wait_ge(qk_copied[0], B + 1)

            def attend(i, last):
                for s in range(SLOTS - GROUP if last else SLOTS):
                    more = not (last and s + AHEAD_S >= SLOTS)
                    if more:
                        scores(i, s + AHEAD_S, 0)
                        scores(i, s + AHEAD_S, 1)
                    weigh(i, s)
                    if more:
                        scores(i, s + AHEAD_S, 2)
                    turn_scores(i, s + AHEAD_T, 0)
                    if more:
                        scores(i, s + AHEAD_S, 3)
                    for k in range(1, TT):
                        turn_scores(i, s + AHEAD_T, k)

            turns(pe, TURNS, attend)

            def project_out(b):
                pe.wait_ge(n_low, b + 1)
                by_tokens(0, n_h, n_l, 3).then_inc(proj_done, 1)

            def turn_normalised(b):
                pe.wait_ge(xn3_done, b + 1)
                for j in range(J):
                    for t in range(TT):
                        ins = nc.tensor.transpose(ps[:, 2 + j, t * P:(t + 1) * P], xn3[:, t, j * P:(j + 1) * P], ident[:, :])
                    ins.then_inc(xn3_turned, 1)

            def rank(b):
                pe.wait_ge(xnT_low, J * (b + 1))
                three([(u1_h[:, j, :], u1_l[:, j, :], xnT_h[:, j, :], xnT_l[:, j, :]) for j in range(J)], ps[:, 6, :]).then_inc(rank_done, 1)

            def up(b, f):
                for n, v1 in enumerate((v1_h, v1_l)):
                    ins = nc.tensor.matmul(ps[:, 4 + f % FF_BANKS, :], v1[:, f * P:(f + 1) * P], pT[:, :], start=(n == 0), stop=(n == 1))
                ins.then_inc(ff_done, 1)

            def down(b, f):
                pe.wait_ge(gelu_done, FJ * b + f + 1)
                lo = RANK * (f % 2)
                return nc.tensor.matmul(ps[lo:lo + RANK, 7, :], u2_sb[:, f, :], hT[:, f, :], start=(f < 2), stop=(f >= FJ - 2))

            pe.wait_ge(biased, TT * B * H)
            project_out(0)
            for s in range(SLOTS - GROUP, SLOTS):
                weigh(TURNS - 1, s)
            pe.wait_ge(x1_done, 1)
            pe.wait_ge(n_low, 2)
            by_tokens(0, n_h, n_l, 3, tiles=range(TT // 2))
            pe.wait_ge(exp_done, 2 * B * H)
            turn_normalised(0)
            by_tokens(0, n_h, n_l, 3, tiles=range(TT // 2, TT)).then_inc(proj_done, 1)
            pe.wait_ge(o_read, 2 + 2 * H)
            rank(0)

            def finish(i, last):
                for u in range(2):
                    b, more = 2 * i + u, not (last and u == 1)
                    pe.wait_ge(rank_low, b + 1)
                    for f in range(FJ):
                        up(b, f)
                        if f >= FF_BANKS - 1:
                            down(b, f - FF_BANKS + 1)
                    for f in range(FJ - FF_BANKS + 1, FJ):
                        ins = down(b, f)
                    ins.then_inc(down_done, 1)
                    if more:
                        turn_normalised(b + 1)
                        pe.wait_ge(x1_done, b + 2)
                    else:
                        pe.wait_ge(y_done, 2 * b)
                    pe.wait_ge(down_copied, b + 1)
                    for t in range(TT):
                        ins = nc.tensor.matmul(ps[:, t // 2, (t % 2) * D:(t % 2 + 1) * D], rT[:, t * P:(t + 1) * P], v2_sb[:, :], start=True, stop=True)
                        if t % 2:
                            ins.then_inc(ffn_done, 1)
                    if more:
                        rank(b + 1)
                    if not last:
                        pe.wait_ge(y_done, 2 * (b + 1))
                        project_out(b + 2)

            turns(pe, B // 2, finish)


_INS = ['x', 'ctx_1024', 'mask_BxS2_bk1', 'g_xattn', 'g_ffn', 'L0_xattn_relative_bias', 'L0_xattn_Wq', 'L0_xattn_bq',
        'L0_xattn_Wk', 'L0_xattn_bk', 'L0_xattn_Wv', 'L0_xattn_bv', 'L0_xattn_Wo', 'L0_xattn_bo',
        'L0_ffn_U1', 'L0_ffn_V1', 'L0_ffn_b1', 'L0_ffn_U2', 'L0_ffn_V2', 'L0_ffn_b2']


def kernel(**inputs):
    import numpy as _np
    import concourse.bacc as _bacc
    from concourse import mybir as _mybir
    from concourse.bass_utils import run_bass_kernel_spmd as _run

    nc = _bacc.Bacc("TRN2", target_bir_lowering=False, num_devices=1)
    arrays, args = {}, {}
    for name in _INS:
        a = _np.ascontiguousarray(inputs[name])
        arrays[f"in_{name}_dram"] = a
        args[name] = nc.dram_tensor(f"in_{name}_dram", a.shape, _mybir.dt.from_np(a.dtype), kind="ExternalInput").ap()
    out = nc.dram_tensor("out_0_dram", (B, S, D), F32, kind="ExternalOutput").ap()
    qk_parts = nc.dram_tensor("qk_parts_dram", (2, 3, D, B * S), BF16, kind="Internal").ap()
    values = nc.dram_tensor("values_dram", (B, D, S), F32, kind="Internal").ap()
    flamingo_kernel(nc, *[args[n] for n in _INS], out, qk_parts, values)
    r = _run(nc, [arrays], core_ids=[0])
    return r.results[0]["out_0_dram"]
```
